# Optimizing a Trainium2 kernel written in Bass

```python
import numpy as np
import jax
import jax.numpy as jnp

def _softmax(x, axis=-1):
    return jax.nn.softmax(x, axis=axis)

def _gelu(x):
    return jax.nn.gelu(x, approximate=True)

def _silu(x):
    return jax.nn.silu(x)

def _sigmoid(x):
    return jax.nn.sigmoid(x)

def _layernorm(x, axis=-1, eps=1e-05):
    m = jnp.mean(x, axis=axis, keepdims=True)
    v = jnp.var(x, axis=axis, keepdims=True)
    return (x - m) / jnp.sqrt(v + eps)

def _scatter_add(tgt, idx, src, axis=0):
    return tgt.at[idx].add(src)

def _segment_sum(src, seg, n):
    return jax.ops.segment_sum(src, seg, n)
kernel_name = 'mk_macaron_d1_jaxref_r8_1e36f4'

def setup_inputs(seed: int=0):
    np.random.seed(seed)
    _w = jnp.asarray

    def _L0_attn_setup():
        import jax, jax.numpy as jnp
        import numpy as np
        from math import sqrt
        DIM, RANK, NHEADS = (128, 64, 16)
        B, T = (2, 256)
        key = jax.random.key(seed)
        kx, kq, kk, kv = jax.random.split(key, 4)
        QK_a = sqrt(6.0 / (RANK + DIM))
        VO_a = sqrt(6.0 / (NHEADS * DIM + DIM))
        x = jax.random.normal(kx, (B, T, DIM), dtype=jnp.float32)
        Q = jax.random.uniform(kq, (NHEADS, RANK, DIM), jnp.float32, -QK_a, QK_a)
        K = jax.random.uniform(kk, (NHEADS, RANK, DIM), jnp.float32, -QK_a, QK_a)
        VO = jax.random.uniform(kv, (NHEADS, DIM, DIM), jnp.float32, -VO_a, VO_a)
        return {'x': x, 'Q': Q, 'K': K, 'VO': VO}
    _L0_attn_in = _L0_attn_setup()

    def _L0_ffn_setup():
        import jax, jax.numpy as jnp
        import numpy as np
        GROUP = 16
        EPS = 1e-05

        def _dequant(q, scale):
            w = q.astype(jnp.float32) / 7.5 - 1.0
            return w * jnp.repeat(scale, GROUP, axis=1)

        def _qlora_linear(x, q, scale, bias, la, lb):
            w = _dequant(q, scale)
            base = jnp.einsum('btd,od->bto', x, w) + bias
            lora = jnp.einsum('btr,or->bto', jnp.einsum('btd,rd->btr', x, la), lb)
            return base + lora

        def _layernorm(x, g, b):
            mu = jnp.mean(x, axis=-1, keepdims=True)
            var = jnp.mean(jnp.square(x - mu), axis=-1, keepdims=True)
            return (x - mu) * jax.lax.rsqrt(var + EPS) * g + b
        key = jax.random.key(seed)
        ks = jax.random.split(key, 6)
        D, R, B, T = (128, 32, 8, 512)
        x = jax.random.normal(ks[0], (B, T, D), dtype=jnp.float32)
        qweights = jax.random.randint(ks[1], (6, D, D), 0, 16, dtype=jnp.int32)
        scales = jax.random.uniform(ks[2], (6, D, D // GROUP), dtype=jnp.float32)
        biases = jax.random.normal(ks[3], (6, D), dtype=jnp.float32) * 0.02
        lora_a = jax.random.normal(ks[4], (6, R, D), dtype=jnp.float32) * 0.02
        lora_b = jax.random.normal(ks[5], (6, D, R), dtype=jnp.float32) * 0.02
        ln_gamma = jnp.ones((3, D), dtype=jnp.float32)
        ln_beta = jnp.zeros((3, D), dtype=jnp.float32)
        return {'x': x, 'qweights': qweights, 'scales': scales, 'biases': biases, 'lora_a': lora_a, 'lora_b': lora_b, 'ln_gamma': ln_gamma, 'ln_beta': ln_beta}
    _L0_ffn_in = _L0_ffn_setup()
    _d = {'L0_attn_x': _L0_attn_in['x'], 'L0_attn_Q': _L0_attn_in['Q'], 'L0_attn_K': _L0_attn_in['K'], 'L0_attn_VO': _L0_attn_in['VO'], 'L0_ffn_qweights': _L0_ffn_in['qweights'], 'L0_ffn_scales': _L0_ffn_in['scales'], 'L0_ffn_biases': _L0_ffn_in['biases'], 'L0_ffn_lora_a': _L0_ffn_in['lora_a'], 'L0_ffn_lora_b': _L0_ffn_in['lora_b'], 'L0_ffn_ln_gamma': _L0_ffn_in['ln_gamma'], 'L0_ffn_ln_beta': _L0_ffn_in['ln_beta']}
    _x0 = _d['L0_attn_x']
    _d['L0_attn_x'] = jax.random.normal(jax.random.fold_in(jax.random.key(seed), 1), (8, 512, 128), dtype=_x0.dtype)
    del _x0
    return _d

def reference(L0_attn_x, L0_attn_Q, L0_attn_K, L0_attn_VO, L0_ffn_qweights, L0_ffn_scales, L0_ffn_biases, L0_ffn_lora_a, L0_ffn_lora_b, L0_ffn_ln_gamma, L0_ffn_ln_beta):

    def _L0_attn_ref(x, Q, K, VO):
        import jax, jax.numpy as jnp
        import numpy as np
        from math import sqrt
        DIM, RANK, NHEADS = (128, 64, 16)
        B, T = (2, 256)
        dim = x.shape[-1]
        xq = jnp.einsum('btd,hrd->bthr', x, Q)
        xk = jnp.einsum('bud,hrd->buhr', x, K)
        scores = jnp.einsum('bthr,buhr->bthu', xq, xk) / sqrt(dim)
        attn = jax.nn.softmax(scores, axis=3)
        return jnp.einsum('bthu,bud,hde->bte', attn, x, VO)

    def _L0_ffn_ref(x, qweights, scales, biases, lora_a, lora_b, ln_gamma, ln_beta):
        import jax, jax.numpy as jnp
        import numpy as np
        GROUP = 16
        EPS = 1e-05

        def _dequant(q, scale):
            w = q.astype(jnp.float32) / 7.5 - 1.0
            return w * jnp.repeat(scale, GROUP, axis=1)

        def _qlora_linear(x, q, scale, bias, la, lb):
            w = _dequant(q, scale)
            base = jnp.einsum('btd,od->bto', x, w) + bias
            lora = jnp.einsum('btr,or->bto', jnp.einsum('btd,rd->btr', x, la), lb)
            return base + lora

        def _layernorm(x, g, b):
            mu = jnp.mean(x, axis=-1, keepdims=True)
            var = jnp.mean(jnp.square(x - mu), axis=-1, keepdims=True)
            return (x - mu) * jax.lax.rsqrt(var + EPS) * g + b
        h = x
        for blk in range(3):
            i0, i1 = (2 * blk, 2 * blk + 1)
            y = _qlora_linear(h, qweights[i0], scales[i0], biases[i0], lora_a[i0], lora_b[i0])
            y = _layernorm(y, ln_gamma[blk], ln_beta[blk])
            y = jax.nn.gelu(y, approximate=False)
            y = _qlora_linear(y, qweights[i1], scales[i1], biases[i1], lora_a[i1], lora_b[i1])
            h = y + h
        return h
    x = L0_attn_x
    x = x + 0.5 * _L0_ffn_ref(_layernorm(x, axis=-1), L0_ffn_qweights, L0_ffn_scales, L0_ffn_biases, L0_ffn_lora_a, L0_ffn_lora_b, L0_ffn_ln_gamma, L0_ffn_ln_beta)
    x = x + _L0_attn_ref(_layernorm(x, axis=-1), L0_attn_Q, L0_attn_K, L0_attn_VO)
    x = x + 0.5 * _L0_ffn_ref(_layernorm(x, axis=-1), L0_ffn_qweights, L0_ffn_scales, L0_ffn_biases, L0_ffn_lora_a, L0_ffn_lora_b, L0_ffn_ln_gamma, L0_ffn_ln_beta)
    return x

_drawn_inputs = setup_inputs


def setup_inputs(seed=0):
    import zlib

    import numpy as np

    out = dict(_drawn_inputs(seed))
    spreads = {'L0_ffn_ln_gamma': (1.0, 0.2), 'L0_ffn_ln_beta': (0.0, 0.1)}
    factors = {'L0_ffn_biases': 4.573, 'L0_ffn_lora_a': 5.124, 'L0_ffn_lora_b': 5.261}
    for name, (base, spread) in spreads.items():
        noise = np.random.default_rng([zlib.crc32(name.encode()), seed]).standard_normal(out[name].shape)
        drawn = base * np.exp(spread * noise) if base else spread * noise
        out[name] = jnp.asarray(drawn.astype(out[name].dtype))
    for name, factor in factors.items():
        out[name] = (out[name] * factor).astype(out[name].dtype)
    return out
```

```python
import concourse.bass as bass
from concourse import mybir
from contextlib import ExitStack

F32 = mybir.dt.float32
F16 = mybir.dt.float16
I32 = mybir.dt.int32
ALU = mybir.AluOpType
ACT = mybir.ActivationFunctionType
AX = mybir.AxisListType
RMAX = bass.bass_isa.ReduceOp.max


def macaron(nc, x_d, q_d, k_d, vo_d, qw_d, sc_d, bias_d, la_d, lb_d, gam_d, bet_d, out_d):
    B, T, D = x_d.shape
    H = vo_d.shape[0]
    R = q_d.shape[1] // H
    NL = qw_d.shape[1]
    NB = NL // 2
    G = sc_d.shape[0]
    LR = la_d.shape[0]
    TT = T // 128
    NT = B * TT
    GT = 2 * TT
    GW = GT * 128
    NG = B // 4
    NH = B * H
    RW = D + 1
    LN_EPS = 1e-5
    MAGIC = float(0x5F3759DF)
    EXPONENT = 0x7F800000
    ONE_BITS2 = float(254 << 23)
    QK_TOP = 2.0 ** -4
    VO_CLAMP = 2.0 ** 14

    ctx = ExitStack()
    with ctx:
        def sb(name, shape, dt=F32):
            return ctx.enter_context(nc.sbuf_tensor(name, shape, dt))

        def sem(name):
            return ctx.enter_context(nc.semaphore(name))

        x = sb("x", [128, NT, D])
        ident = sb("ident", [128, 128])
        ident16 = sb("ident16", [128, 128], F16)
        mean_mat = sb("mean_mat", [128, 128])
        ones_col = sb("ones_col", [128, 1])
        qw = sb("qw", [128, NL, D], I32)
        scl = sb("scl", [128, NL, D])
        la = sb("la", [LR, NL, D])
        lb = sb("lb", [LR, NL, D])
        wt = sb("wt", [128, NL, D])
        wmean = sb("wmean", [128, NL])
        bias = sb("bias", [128, NL])
        bias_c = sb("bias_c", [128, NL])
        gam = sb("gam", [128, NB])
        bet = sb("bet", [128, NB])

        qk32 = sb("qk32", [128, 2, H * R])
        vo32 = sb("vo32", [128, H, D])
        vo_last = sb("vo_last", [128, H, D])
        w_hi = sb("w_hi", [128, 2, H * R], F16)
        w_lo = sb("w_lo", [128, 2, H * R], F16)
        vo_hi = sb("vo_hi", [128, H, RW + 1], F16)
        vo_lo = sb("vo_lo", [128, H, D], F16)
        amax = sb("amax", [128, 4])
        pow2 = sb("pow2", [128, 4])
        inv2 = sb("inv2", [128, 4])
        exp_scale = sb("exp_scale", [128, 1])

        xn_hi = sb("xn_hi", [128, NT, D], F16)
        xn_lo = sb("xn_lo", [128, NT, D], F16)
        xt_hi = sb("xt_hi", [128, B, T], F16)
        xt_lo = sb("xt_lo", [128, B, T], F16)

        stats = sb("stats", [128, 2, GT, 6])
        mv = sb("mv", [128, 2, GT, 2])
        var = sb("var", [128, 2, GT])
        rs_t = sb("rs_t", [128, 2, GT])
        rs_u = sb("rs_u", [128, 2, GT])
        rstd = sb("rstd", [128, 2, GT])
        xhat = sb("xhat", [128, 2, GT, D])
        hT = sb("hT", [128, 2, GW])
        yc = sb("yc", [128, 2, GW])
        shared = sb("shared", [128, 2, 2, GW])
        sq = shared[:, 0, :, :]
        z = shared[:, 1, :, :]
        gl = sb("gl", [128, 2, GW])

        qh_pair = sb("qh_pair", [128, T], F16)
        ql_pair = sb("ql_pair", [128, T], F16)
        kh_pair = sb("kh_pair", [128, T], F16)
        kl_pair = sb("kl_pair", [128, T], F16)
        RING = 4
        q1 = sb("q1", [128, RING, T], F16)
        q2 = sb("q2", [128, RING, T], F16)
        k1 = sb("k1", [128, RING, T], F16)
        k2 = sb("k2", [128, RING, T], F16)
        mcol = sb("mcol", [128, 2, TT, 128], F16)
        p32 = shared[:, :, :, :].rearrange("p a g (t n) -> p a (g t) n", n=T)
        p_hi = sb("p_hi", [128, 2, TT, T], F16)
        p_lo = sb("p_lo", [128, 2, TT, T], F16)
        y_hi = sb("y_hi", [128, T], F16)
        y_lo = sb("y_lo", [128, T], F16)
        rinv = sb("rinv", [128, TT])

        ps = ctx.enter_context(nc.psum_tensor("ps", [128, 8, 512], F32))
        lin_ps = [ps[:, 4 * g:4 * g + 2, :].rearrange("p a b -> p (a b)") for g in range(2)]
        rb_ps = [ps[:, 4 * g + 2:4 * g + 4, :].rearrange("p a b -> p (a b)") for g in range(2)]
        s_ps = [ps[:, 2 * a:2 * a + 2, :] for a in range(2)]
        y_ps = ps[:, 4, :]
        pj_ps = ps[:, 5, :]
        o_ps = ps[:, 6:8, 0:2 * RW].rearrange("p b (t n) -> p b t n", n=RW)

        vch = sem("vch")
        s_done = sem("s_done")
        x_in = [sem(f"x_in{g}") for g in range(2 * NG)]
        w_in = sem("w_in")
        sc_in = sem("sc_in")
        a_in = sem("a_in")
        consts = sem("consts")
        prep_pe = sem("prep_pe")
        prep_v = sem("prep_v")
        prep_a = sem("prep_a")
        prep_p = sem("prep_p")
        xhat_ready = sem("xhat_ready")
        pre_t = sem("pre_t")
        h_ready = sem("h_ready")
        lin1_done = sem("lin1_done")
        yc_ready = sem("yc_ready")
        sq_ready = sem("sq_ready")
        var_done = sem("var_done")
        rstd_ready = sem("rstd_ready")
        rb_done = sem("rb_done")
        z_ready = sem("z_ready")
        gl_ready = sem("gl_ready")
        lin2_done = sem("lin2_done")
        post_t = sem("post_t")
        x1_ready = sem("x1_ready")
        xn_ready = sem("xn_ready")
        xn_t = sem("xn_t")
        xnh_ready = sem("xnh_ready")
        xth_ready = sem("xth_ready")
        xsplit_done = sem("xsplit_done")
        xcol_ready = sem("xcol_ready")
        out_sem = sem("out_sem")

        q_proj = sem("q_proj")
        k_proj = sem("k_proj")
        qh_ready = sem("qh_ready")
        ql_ready = sem("ql_ready")
        kh_ready = sem("kh_ready")
        kl_ready = sem("kl_ready")
        q_spread = sem("q_spread")
        k_spread = sem("k_spread")
        max_mm = sem("max_mm")
        max_red = sem("max_red")
        m_turned = sem("m_turned")
        m_ready = sem("m_ready")
        exp_done = sem("exp_done")
        phi_done = sem("phi_done")
        plo_done = sem("plo_done")
        av_half = sem("av_half")
        yh_ready = sem("yh_ready")
        yl_ready = sem("yl_ready")
        o_done = sem("o_done")
        o_added = sem("o_added")

        block = ctx.enter_context(nc.Block())

        class Link:
            def __init__(self):
                self.base, self.n = 0, 0

            def __call__(self, eng, ins, alone=False):
                self.n += 1
                ins.then_inc(vch, 1)
                if alone:
                    value = eng.to_reg(self.base + self.n)
                    eng.wait_ge(w_in, 16)
                    eng.wait_ge(vch, value)
                else:
                    eng.wait_ge(vch, self.base + self.n)

        @block.sync
        def _(sp):
            xv = x_d.rearrange("b (n p) d -> p (b n) d", p=128)
            sp.dma_start(x[:, 0:GT, :], xv[:, 0:GT, :]).then_inc(x_in[0], 16)
            sp.dma_start(x[:, GT:2 * GT, :], xv[:, GT:2 * GT, :]).then_inc(x_in[1], 16)
            sp.dma_start(qw[:, :, :], qw_d).then_inc(w_in, 16)
            sp.dma_start(la[:, :, :], la_d).then_inc(w_in, 16)
            sp.dma_start(lb[:, :, :], lb_d).then_inc(w_in, 16)
            sp.dma_start(bias[:, :], bias_d).then_inc(w_in, 16)
            sp.dma_start(gam[:, :], gam_d).then_inc(w_in, 16)
            sp.dma_start(bet[:, :], bet_d).then_inc(w_in, 16)
            for g in range(2, 2 * NG):
                sp.dma_start(x[:, g * GT:(g + 1) * GT, :], xv[:, g * GT:(g + 1) * GT, :]).then_inc(x_in[g], 16)
            sp.dma_start(qk32[:, 0, :], q_d).then_inc(a_in, 16)
            sp.dma_start(qk32[:, 1, :], k_d).then_inc(a_in, 16)
            sp.dma_start(vo32[:, :, :], vo_d.rearrange("h d e -> d h e")).then_inc(a_in, 16)
            sp.dma_start(vo_last[:, :, :], vo_d[:, D - 1, :].partition_broadcast(128)).then_inc(a_in, 16)

            def spread(ready, ring):
                def spread_q():
                    sp.wait_ge(qh_ready, ready)
                    sp.wait_ge(ql_ready, ready)
                    for e in range(2):
                        half = slice(64 * e, 64 * e + 64)
                        sp.dma_start(q1[0:64, ring + e, :], qh_pair[half, :]).then_inc(q_spread, 16)
                        sp.dma_start(q1[64:128, ring + e, :], qh_pair[half, :]).then_inc(q_spread, 16)
                        sp.dma_start(q2[0:64, ring + e, :], ql_pair[half, :]).then_inc(q_spread, 16)

                def spread_k():
                    sp.wait_ge(kh_ready, ready)
                    sp.wait_ge(kl_ready, ready)
                    for e in range(2):
                        half = slice(64 * e, 64 * e + 64)
                        sp.dma_start(k1[0:64, ring + e, :], kh_pair[half, :]).then_inc(k_spread, 16)
                        sp.dma_start(k2[0:64, ring + e, :], kh_pair[half, :]).then_inc(k_spread, 16)
                        sp.dma_start(k1[64:128, ring + e, :], kl_pair[half, :]).then_inc(k_spread, 16)
                spread_q()
                spread_k()

            sp.wait_ge(prep_v, 4)
            spread(1, 0)
            spread(2, 2)
            with sp.Fori(0, NH // 4 - 1) as i:
                used = [sp.to_reg(8 * i + 4 * (j + 1)) for j in range(2)]
                ready = [sp.to_reg(2 * i + (j + 3)) for j in range(2)]
                for j in range(2):
                    sp.wait_ge(prep_v, 4)
                    sp.wait_ge(s_done, used[j])
                    spread(ready[j], 2 * j)

            ov = out_d.rearrange("b (n p) d -> p (b n) d", p=128)
            for g in range(2 * NG):
                sp.wait_ge(x1_ready, 2 * NG + g + 1)
                sp.dma_start(ov[:, g * GT:(g + 1) * GT, :], x[:, g * GT:(g + 1) * GT, :]).then_inc(out_sem, 16)
            sp.wait_ge(out_sem, 16 * 2 * NG)

        @block.gpsimd
        def _(pool):
            pool.memset(ident[:, :], 0.0).then_inc(prep_p, 1)
            pool.memset(mean_mat[:, :], 1.0 / D).then_inc(consts, 1)
            pool.memset(ones_col[:, :], 1.0 / D).then_inc(consts, 1)
            pool.wait_ge(prep_p, 1)
            pool.affine_select(out=ident[:, :], in_=ident[:, :], compare_op=ALU.not_equal, fill=1.0,
                               base=0, pattern=[[-1, 128]], channel_multiplier=1).then_inc(consts, 1)
            pool.wait_ge(prep_v, 2)
            pool.partition_all_reduce(pow2[:, 0:3], amax[:, 0:3], 128, RMAX).then_inc(prep_p, 1)

            pool.memset(xn_hi[:, :, D - 1:D], 1.0).then_inc(xcol_ready, 1)
            pool.memset(xn_lo[:, :, D - 1:D], 0.0).then_inc(xcol_ready, 1)

            def p_low(k, par, a):
                pool.wait_ge(phi_done, 2 * k + (a + 1))
                rows = slice(2 * a, 2 * a + 2)
                pool.tensor_tensor(p_lo[:, par, rows, :], p32[:, par, rows, :], p_hi[:, par, rows, :],
                                   ALU.subtract).then_inc(plo_done, 1)

            for a in range(2):
                p_low(0, 0, a)
            for a in range(2):
                p_low(1, 1, a)
            with pool.Fori(0, NH // 2 - 1) as i:
                for j in range(2):
                    k = 2 * i + (j + 2)
                    for a in range(2):
                        pool.wait_ge(av_half, 2 * (k - 2) + (a + 1))
                        p_low(k, j, a)

        @block.scalar
        def _(act):
            act.dma_start(scl[0:16, :, :], sc_d[0].partition_broadcast(16)).then_inc(sc_in, 16)
            for s in range(1, G):
                act.dma_start(scl[16 * s:16 * s + 16, :, :], sc_d[s].partition_broadcast(16)).then_inc(sc_in, 16)

            act.wait_ge(consts, 3)
            nc.scalar.activation(ident16[:, :], ident[:, :], ACT.Copy).then_inc(prep_a, 1)

            def ffn(f):
                with act.Fori(0, NG) as it:
                    pre = 2 * it + 2 * NG * f
                    stp = 2 * NB * it + 2 * NB * NG * f
                    for g in range(2):
                        act.wait_ge(pre_t, pre + (g + 1))
                        nc.scalar.activation(hT[:, g, :], lin_ps[g], ACT.Copy).then_inc(h_ready, 1)

                    def centre(g, n):
                        blk = n
                        act.wait_ge(lin1_done, stp + (2 * blk + g + 1))
                        nc.scalar.activation(yc[:, g, :], lin_ps[g], ACT.Identity,
                                             bias=bias_c[:, 2 * blk:2 * blk + 1]).then_inc(yc_ready, 1)
                        nc.scalar.activation(sq[:, g, :], lin_ps[g], ACT.Square,
                                             bias=bias_c[:, 2 * blk:2 * blk + 1]).then_inc(sq_ready, 1)

                    def gelu(g, n):
                        act.wait_ge(z_ready, stp + (2 * n + g + 1))
                        nc.scalar.activation(gl[:, g, :], z[:, g, :], ACT.Gelu, scale=gam[:, n:n + 1],
                                             bias=bet[:, n:n + 1]).then_inc(gl_ready, 1)

                    centre(0, 0)
                    for n in range(NB):
                        centre(1, n)
                        gelu(0, n)
                        if n + 1 < NB:
                            centre(0, n + 1)
                        gelu(1, n)
                    if f == 0:
                        for g in range(2):
                            act.wait_ge(xn_ready, pre + (g + 1))
                            nc.scalar.activation(xn_hi[:, bass.ds(it * (2 * GT) + g * GT, GT), 0:D - 1],
                                                 xhat[:, g, :, 0:D - 1], ACT.Copy).then_inc(xnh_ready, 1)
                            act.wait_ge(xn_t, pre + (g + 1))
                            nc.scalar.activation(
                                xt_hi[:, bass.ds(it * 4 + 2 * g, 2), :].rearrange("p a b -> p (a b)"),
                                rb_ps[g], ACT.Copy).then_inc(xth_ready, 1)

            act.wait_ge(prep_v, 3)
            nc.scalar.activation(w_hi[:, :, :], qk32[:, :, :], ACT.Copy).then_inc(prep_a, 1)
            nc.scalar.activation(vo_hi[:, :, 0:D], vo32[:, :, :], ACT.Copy).then_inc(prep_a, 1)
            ffn(0)

            def q_high(pair):
                act.wait_ge(q_proj, pair + 1)
                nc.scalar.activation(qh_pair[:, :], pj_ps, ACT.Copy).then_inc(qh_ready, 1)

            def k_high(pair):
                act.wait_ge(k_proj, pair + 1)
                nc.scalar.activation(kh_pair[:, :], pj_ps, ACT.Copy).then_inc(kh_ready, 1)

            def row_max(k, ring):
                act.wait_ge(m_turned, k + 1)
                nc.scalar.activation(q2[64:128, ring, :], pj_ps[64:128, :], ACT.Copy).then_inc(m_ready, 1)

            def exps(k, par, a):
                act.wait_ge(s_done, 2 * k + (a + 1))
                nc.scalar.activation(p32[:, par, 2 * a:2 * a + 2, :], s_ps[a], ACT.Exp,
                                     scale=exp_scale[:, 0:1]).then_inc(exp_done, 1)

            def p_high(k, par, a):
                act.wait_ge(exp_done, 2 * k + (a + 1))
                nc.scalar.activation(p_hi[:, par, 2 * a:2 * a + 2, :], p32[:, par, 2 * a:2 * a + 2, :],
                                     ACT.Copy).then_inc(phi_done, 1)

            def y_high(k):
                act.wait_ge(av_half, 2 * k + 2)
                nc.scalar.activation(y_hi[:, :], y_ps, ACT.Copy).then_inc(yh_ready, 1)

            def spread_over(pair):
                act.wait_ge(q_spread, 96 * pair)
                act.wait_ge(k_spread, 96 * pair)

            def slot(k, j, lo, hi):
                if lo >= -1 and hi + 1 < NH:
                    if lo + 1 >= 2:
                        act.wait_ge(plo_done, 2 * (k - 1) + 1)
                        act.wait_ge(av_half, 2 * (k - 1) + 1)
                    exps(k + 1, (j + 1) % 2, 0)
                    p_high(k + 1, (j + 1) % 2, 0)
                if lo >= -2 and hi + 2 < NH:
                    row_max(k + 2, (j + 2) % 4)
                if lo >= -1 and hi + 1 < NH:
                    if lo + 1 >= 2:
                        act.wait_ge(plo_done, 2 * (k - 1) + 2)
                        act.wait_ge(av_half, 2 * (k - 1) + 2)
                    exps(k + 1, (j + 1) % 2, 1)
                if lo >= 0:
                    if lo >= 1:
                        act.wait_ge(o_done, k)
                    y_high(k)
                if lo >= -1 and hi + 1 < NH:
                    p_high(k + 1, (j + 1) % 2, 1)
                if j % 2 == 0 and hi + 4 < NH:
                    pair = (k + 4) // 2 if isinstance(k, int) else pair_of(k, j)
                    if lo > -4:
                        spread_over(pair)
                    q_high(pair)
                    k_high(pair)

            quad = [None]

            def pair_of(k, j):
                return 2 * quad[0] + (j // 2 + 2)

            for k in range(-4, 0):
                slot(k, k % 4, k, k)
            for k in range(0, 4):
                slot(k, k % 4, k, k)
            with act.Fori(1, NH // 4 - 1) as i:
                quad[0] = i
                for j in range(4):
                    slot(4 * i + j, j, 4 + j, NH - 8 + j)
            for k in range(NH - 4, NH):
                slot(k, k % 4, k, k)

            ffn(1)

        @block.vector
        def _(dve):
            link = Link()

            def rsqrt(link, eps, src, g):
                v, t, u, y = var[:, g, :], rs_t[:, g, :], rs_u[:, g, :], rstd[:, g, :]
                link(dve, nc.vector.tensor_scalar(v, src, eps, None, ALU.add))
                link(dve, nc.vector.tensor_scalar(y.bitcast(I32), v.bitcast(I32), -0.5, MAGIC, ALU.mult, ALU.add))
                for step in range(4):
                    link(dve, nc.vector.scalar_tensor_tensor(t, y, -0.5, y, ALU.mult, ALU.mult))
                    link(dve, nc.vector.tensor_tensor(u, t, v, ALU.mult))
                    last = nc.vector.scalar_tensor_tensor(y, u, 1.5, y, ALU.add, ALU.mult)
                    if step < 3:
                        link(dve, last)
                return last

            dve.wait_ge(w_in, 16 * 6)
            link(dve, nc.vector.tensor_scalar(wt[:, :, :], qw[:, :, :], 1.0 / 7.5, -1.0, ALU.mult, ALU.add))
            dve.wait_ge(sc_in, 16 * G)
            link(dve, nc.vector.tensor_tensor(wt[:, :, :], wt[:, :, :], scl[:, :, :], ALU.mult))
            dve.wait_ge(prep_pe, 1)
            for b in range(2):
                half = slice(3 * b, 3 * b + 3)
                ins = nc.vector.tensor_tensor(
                    wt[:, half, :], ps[:, b, 0:3 * D].rearrange("p (n d) -> p n d", n=3), wt[:, half, :], ALU.add)
                link(dve, ins)
            link(dve, nc.vector.tensor_reduce(wmean[:, :], wt[:, :, :], AX.X, ALU.add))
            link(dve, nc.vector.tensor_scalar(wmean[:, :], wmean[:, :], -1.0 / D, None, ALU.mult))
            for n in range(0, NL, 2):
                link(dve, nc.vector.tensor_scalar(wt[:, n, :], wt[:, n, :], wmean[:, n:n + 1], None, ALU.add))
            link(dve, nc.vector.tensor_copy(bias_c[:, :], bias[:, :]))
            nc.vector.tensor_tensor(bias_c[:, 0:NL:2], bias[:, 0:NL:2], ps[:, 2, 0:NL:2],
                                    ALU.subtract).then_inc(prep_v, 1)

            dve.wait_ge(a_in, 16 * 4)
            link(dve, nc.vector.tensor_tensor(vo32[:, :, :], vo32[:, :, :], vo_last[:, :, :], ALU.subtract))
            for n, w in enumerate((qk32[:, 0, :], qk32[:, 1, :], vo32[:, :, :].rearrange("p h d -> p (h d)"))):
                ins = nc.vector.tensor_reduce(amax[:, n:n + 1], w, AX.X, ALU.max, apply_absolute_value=True)
                link(dve, ins)
            nc.vector.tensor_scalar(amax[:, 0:3], amax[:, 0:3], 1e-30, None, ALU.max).then_inc(prep_v, 1)
            dve.wait_ge(prep_p, 2)
            link(dve, nc.vector.tensor_scalar(pow2[:, 0:3].bitcast(I32), pow2[:, 0:3].bitcast(I32), EXPONENT, None,
                                              ALU.bitwise_and))
            link(dve, nc.vector.tensor_scalar(inv2[:, 0:3].bitcast(I32), pow2[:, 0:3].bitcast(I32), -1.0, ONE_BITS2,
                                              ALU.mult, ALU.add))
            link(dve, nc.vector.tensor_scalar(inv2[:, 2:3], inv2[:, 2:3], VO_CLAMP, 1.0 / VO_CLAMP,
                                              ALU.min, ALU.max))
            link(dve, nc.vector.tensor_scalar(exp_scale[:, :], pow2[:, 0:1], pow2[:, 1:2],
                                              1.0 / (QK_TOP * QK_TOP * float(D) ** 0.5), ALU.mult, ALU.mult))
            for n in range(2):
                link(dve, nc.vector.tensor_scalar(qk32[:, n, :], qk32[:, n, :], inv2[:, n:n + 1], QK_TOP,
                                                  ALU.mult, ALU.mult))
            dve.wait_ge(consts, 3)
            for h in range(H):
                ins = nc.vector.tensor_scalar(vo_hi[:, h, D:D + 1], ident[:, D - 1:D], inv2[:, 2:3], None, ALU.mult)
            link(dve, ins)
            nc.vector.tensor_scalar(vo32[:, :, :], vo32[:, :, :], inv2[:, 2:3], None, ALU.mult).then_inc(prep_v, 1)
            dve.wait_ge(prep_a, 2)
            nc.vector.tensor_tensor(w_lo[:, :, :], qk32[:, :, :], w_hi[:, :, :], ALU.subtract)
            dve.wait_ge(prep_a, 3)
            nc.vector.tensor_tensor(vo_lo[:, :, :], vo32[:, :, :], vo_hi[:, :, 0:D], ALU.subtract)
            nc.vector.memset(mcol[:, :, :, :], 0.0)
            nc.vector.memset(q2[64:128, :, :], 0.0)
            link(dve, nc.vector.memset(k2[64:128, :, :], 0.0))
            nc.vector.memset(k2[64:65, :, :], 1.0).then_inc(prep_v, 1)

            def norm_tokens(link, rows, g, ready):
                for t in range(GT):
                    ins = nc.vector.bn_stats(stats[:, g, t, :], x[:, rows(t, 1), :].rearrange("p a d -> p (a d)"))
                link(dve, ins, alone=True)
                for t in range(GT):
                    ins = nc.vector.bn_aggr(mv[:, g, t, :], stats[:, g, t, :])
                link(dve, ins)
                link(dve, rsqrt(link, LN_EPS, mv[:, g, :, 1], g))
                for t in range(GT):
                    ins = nc.vector.tensor_scalar(xhat[:, g, t, :], x[:, rows(t, 1), :].rearrange("p a d -> p (a d)"),
                                                  mv[:, g, t, 0:1], rstd[:, g, t:t + 1], ALU.subtract, ALU.mult)
                ins.then_inc(ready, 1)

            LN_LINKS = 2 + 14
            STEP_LINKS = 13

            def ffn_phase(f):
                start = link.base + link.n
                per = 2 * LN_LINKS * (2 if f == 0 else 1) + 2 * NB * STEP_LINKS
                if f == 0:
                    for s in x_in:
                        dve.wait_ge(s, 16)
                with dve.Fori(0, NG) as it:
                    mine = Link()
                    mine.base = it * per + start
                    pre = 2 * it + 2 * NG * f
                    stp = 2 * NB * it + 2 * NB * NG * f
                    at = lambda g: (lambda t, n: bass.ds(it * (2 * GT) + (g * GT + t), n))
                    for g in range(2):
                        norm_tokens(mine, at(g), g, xhat_ready)

                    def step_rsqrt(g, n):
                        dve.wait_ge(var_done, stp + (2 * n + g + 1))
                        rsqrt(mine, LN_EPS, rb_ps[g][:, 0:GT], g).then_inc(rstd_ready, 1)

                    def step_z(g, n):
                        dve.wait_ge(yc_ready, stp + (2 * n + g + 1))
                        dve.wait_ge(rb_done, stp + (2 * n + g + 1))
                        nc.vector.tensor_tensor(z[:, g, :], rb_ps[g], yc[:, g, :], ALU.mult).then_inc(z_ready, 1)

                    def step_h(g, n):
                        dve.wait_ge(lin2_done, stp + (2 * n + g + 1))
                        nc.vector.scalar_tensor_tensor(hT[:, g, :], lin_ps[g], bias[:, 2 * n + 1:2 * n + 2],
                                                       hT[:, g, :], ALU.add, ALU.add).then_inc(h_ready, 1)

                    step_rsqrt(0, 0)
                    for n in range(NB):
                        step_z(0, n)
                        step_rsqrt(1, n)
                        step_h(0, n)
                        step_z(1, n)
                        if n + 1 < NB:
                            step_rsqrt(0, n + 1)
                        step_h(1, n)
                    for g in range(2):
                        dve.wait_ge(post_t, pre + (g + 1))
                        rows = x[:, bass.ds(it * (2 * GT) + g * GT, GT), :].rearrange("p a d -> p (a d)")
                        nc.vector.scalar_tensor_tensor(rows, lin_ps[g], 0.5, rows, ALU.mult,
                                                       ALU.add).then_inc(x1_ready, 1)
                        if f == 0:
                            dve.wait_ge(w_in, 16)
                            dve.wait_ge(x1_ready, pre + (g + 1))
                            norm_tokens(mine, at(g), g, xn_ready)
                            dve.wait_ge(xnh_ready, pre + (g + 1))
                            tiles = bass.ds(it * (2 * GT) + g * GT, GT)
                            nc.vector.tensor_tensor(xn_lo[:, tiles, 0:D - 1], xhat[:, g, :, 0:D - 1],
                                                    xn_hi[:, tiles, 0:D - 1], ALU.subtract)
                            dve.wait_ge(xth_ready, pre + (g + 1))
                            two = bass.ds(it * 4 + 2 * g, 2)
                            nc.vector.tensor_tensor(xt_lo[:, two, :].rearrange("p a b -> p (a b)"), rb_ps[g],
                                                    xt_hi[:, two, :].rearrange("p a b -> p (a b)"),
                                                    ALU.subtract).then_inc(xsplit_done, 1)
                    assert mine.n == per, (mine.n, per)
                link.base, link.n = start + NG * per, 0

            ffn_phase(0)

            ADD_LINKS = 1

            def q_low(pair):
                dve.wait_ge(qh_ready, pair + 1)
                nc.vector.tensor_tensor(ql_pair[:, :], pj_ps, qh_pair[:, :], ALU.subtract).then_inc(ql_ready, 1)

            def k_low(pair):
                dve.wait_ge(kh_ready, pair + 1)
                nc.vector.tensor_tensor(kl_pair[:, :], pj_ps, kh_pair[:, :], ALU.subtract).then_inc(kl_ready, 1)

            def reduce_max(k, par, a):
                dve.wait_ge(max_mm, 2 * k + (a + 1))
                nc.vector.tensor_reduce(mcol[:, par, 2 * a:2 * a + 2, R], s_ps[a], AX.X, ALU.max,
                                        negate=True).then_inc(max_red, 1)

            def y_low(k):
                dve.wait_ge(yh_ready, k + 1)
                nc.vector.tensor_tensor(y_lo[:, :], y_ps, y_hi[:, :], ALU.subtract).then_inc(yl_ready, 1)

            def add_out(mine, k, batch):
                dve.wait_ge(o_done, k + 1)
                mine(dve, nc.vector.reciprocal(rinv[:, :].rearrange("p (a b) -> p a b", a=2), o_ps[:, :, :, D]))
                for t in range(TT):
                    row = x[:, bass.ds(batch * TT + t, 1), :].rearrange("p a d -> p (a d)")
                    ins = nc.vector.scalar_tensor_tensor(row, o_ps[:, t // 2, t % 2, 0:D], rinv[:, t:t + 1], row,
                                                         ALU.mult, ALU.add)
                ins.then_inc(o_added, 1)

            def slot(mine, i, k, j, lo, hi):
                if lo >= 0:
                    y_low(k)
                pair = 2 * i + (j // 2 + 2)
                if j % 2 == 0 and hi + 4 < NH:
                    if lo > -4:
                        dve.wait_ge(q_spread, 96 * pair)
                        dve.wait_ge(k_spread, 96 * pair)
                    q_low(pair)
                if lo >= -3 and hi + 3 < NH:
                    if lo + 3 >= 2:
                        dve.wait_ge(m_turned, k + 2)
                    reduce_max(k + 3, (j + 3) % 2, 0)
                if j % 2 == 0 and hi + 4 < NH:
                    k_low(pair)
                if lo >= -3 and hi + 3 < NH:
                    reduce_max(k + 3, (j + 3) % 2, 1)
                if lo >= 0:
                    if lo >= 1:
                        dve.wait_ge(o_added, k)
                    add_out(mine, k, i // (H // 4))

            for k in range(-4, 4):
                slot(link, k // 4, k, k % 4, k, k)
            start = link.base + link.n
            with dve.Fori(1, NH // 4 - 1) as i:
                mine = Link()
                mine.base = i * (4 * ADD_LINKS) + (start - 4 * ADD_LINKS)
                for j in range(4):
                    slot(mine, i, 4 * i + j, j, 4 + j, NH - 8 + j)
            link.base, link.n = start + (NH // 4 - 2) * 4 * ADD_LINKS, 0
            for k in range(NH - 4, NH):
                slot(link, k // 4, k, k % 4, k, k)
            dve.wait_ge(o_added, NH)

            ffn_phase(1)

        @block.tensor
        def _(pe):
            pe.wait_ge(w_in, 16 * 6)
            pe.wait_ge(consts, 3)
            nc.tensor.matmul(ps[:, 2, 0:NL], mean_mat[:, :], bias[:, :], start=True, stop=True)
            for n in range(NL):
                ins = nc.tensor.matmul(ps[:, n // 3, (n % 3) * D:(n % 3 + 1) * D], la[:, n, :], lb[:, n, :],
                                       start=True, stop=True)
            ins.then_inc(prep_pe, 1)
            pe.wait_ge(prep_v, 1)

            def turn(dst, src, tiles):
                for t in range(tiles):
                    ins = nc.tensor.transpose(dst[:, t * 128:(t + 1) * 128], src(t), ident[:, :])
                return ins

            def ffn(f):
                with pe.Fori(0, NG) as it:
                    pre = 2 * it + 2 * NG * f
                    stp = 2 * NB * it + 2 * NB * NG * f
                    hst = 2 * (NB + 1) * it + 2 * (NB + 1) * NG * f

                    def lin1(g, n):
                        pe.wait_ge(h_ready, hst + (2 * n + g + 1))
                        for c in range(2):
                            cols = slice(512 * c, 512 * c + 512)
                            ins = nc.tensor.matmul(lin_ps[g][:, cols], wt[:, 2 * n, :], hT[:, g, cols],
                                                   start=True, stop=True)
                        ins.then_inc(lin1_done, 1)

                    def variance(g, n):
                        pe.wait_ge(sq_ready, stp + (2 * n + g + 1))
                        if n:
                            pe.wait_ge(z_ready, stp + (2 * (n - 1) + g + 1))
                        for t in range(GT):
                            ins = nc.tensor.matmul(rb_ps[g][:, t:t + 1], sq[:, g, t * 128:(t + 1) * 128],
                                                   ones_col[:, :], start=True, stop=True)
                        ins.then_inc(var_done, 1)

                    def spread_rstd(g, n):
                        pe.wait_ge(rstd_ready, stp + (2 * n + g + 1))
                        for t in range(GT):
                            ins = nc.tensor.matmul(rb_ps[g][:, t * 128:(t + 1) * 128],
                                                   rstd[:, g, t:t + 1].to_broadcast([128, 128]), ident[:, :],
                                                   start=True, stop=True)
                        ins.then_inc(rb_done, 1)

                    def lin2(g, n):
                        pe.wait_ge(gl_ready, stp + (2 * n + g + 1))
                        for c in range(2):
                            cols = slice(512 * c, 512 * c + 512)
                            ins = nc.tensor.matmul(lin_ps[g][:, cols], wt[:, 2 * n + 1, :], gl[:, g, cols],
                                                   start=True, stop=True)
                        ins.then_inc(lin2_done, 1)

                    for g in range(2):
                        pe.wait_ge(xhat_ready, pre + (g + 1))
                        turn(lin_ps[g], lambda t: xhat[:, g, t, :], GT).then_inc(pre_t, 1)
                    lin1(0, 0)
                    variance(0, 0)
                    for n in range(NB):
                        spread_rstd(0, n)
                        lin1(1, n)
                        lin2(0, n)
                        variance(1, n)
                        if n + 1 < NB:
                            lin1(0, n + 1)
                        spread_rstd(1, n)
                        if n + 1 < NB:
                            variance(0, n + 1)
                        lin2(1, n)
                    for g in range(2):
                        pe.wait_ge(h_ready, hst + (2 * NB + g + 1))
                        turn(lin_ps[g], lambda t: hT[:, g, t * 128:(t + 1) * 128], GT).then_inc(post_t, 1)
                    if f == 0:
                        for g in range(2):
                            pe.wait_ge(xn_ready, pre + (g + 1))
                            turn(rb_ps[g], lambda t: xhat[:, g, t, :], GT).then_inc(xn_t, 1)

            ffn(0)

            pe.wait_ge(prep_v, 4)
            pe.wait_ge(xcol_ready, 2)
            pe.wait_ge(xsplit_done, 2 * NG)

            def project(which, pair, col, batch, done):
                hi = w_hi[:, which, bass.ds(col, 128)]
                lo = w_lo[:, which, bass.ds(col, 128)]
                xh = xt_hi[:, bass.ds(batch, 1), :].rearrange("p a t -> p (a t)")
                xl = xt_lo[:, bass.ds(batch, 1), :].rearrange("p a t -> p (a t)")
                nc.tensor.matmul(pj_ps, hi, xh, start=True, stop=False)
                nc.tensor.matmul(pj_ps, hi, xl, start=False, stop=False)
                nc.tensor.matmul(pj_ps, lo, xh, start=False, stop=True).then_inc(done, 1)

            def maxima(k, ring, a):
                for t in (2 * a, 2 * a + 1):
                    ins = nc.tensor.matmul(s_ps[a][:, t % 2, :], q1[:, ring, t * 128:(t + 1) * 128], k1[:, ring, :],
                                           start=True, stop=True)
                ins.then_inc(max_mm, 1)

            def turn_max(k, par):
                for t in range(TT):
                    ins = nc.tensor.matmul(pj_ps[:, t * 128:(t + 1) * 128], mcol[:, par, t, :], ident16[:, :],
                                           start=True, stop=True)
                ins.then_inc(m_turned, 1)

            def scores(k, ring, a):
                for u in (2 * a, 2 * a + 1):
                    keys = slice(u * 128, (u + 1) * 128)
                    nc.tensor.matmul(s_ps[a][:, u % 2, :], k1[:, ring, keys], q1[:, ring, :], start=True, stop=False)
                    ins = nc.tensor.matmul(s_ps[a][:, u % 2, :], k2[:, ring, keys], q2[:, ring, :],
                                           start=False, stop=True)
                ins.then_inc(s_done, 1)

            def weigh(par, a, batch):
                for u in (2 * a, 2 * a + 1):
                    row = bass.ds(batch * TT + u, 1)
                    xh = xn_hi[:, row, :].rearrange("p a d -> p (a d)")
                    xl = xn_lo[:, row, :].rearrange("p a d -> p (a d)")
                    nc.tensor.matmul(y_ps, xh, p_hi[:, par, u, :], start=(u == 0), stop=False)
                    nc.tensor.matmul(y_ps, xl, p_hi[:, par, u, :], start=False, stop=False)
                    ins = nc.tensor.matmul(y_ps, xh, p_lo[:, par, u, :], start=False, stop=(u == TT - 1))
                ins.then_inc(av_half, 1)

            def outputs(head):
                vh = vo_hi[:, bass.ds(head, 1), 0:RW].rearrange("p a d -> p (a d)")
                vl = vo_lo[:, bass.ds(head, 1), :].rearrange("p a d -> p (a d)")
                for t in range(TT):
                    cols = slice(t * 128, (t + 1) * 128)
                    o = o_ps[:, t // 2, t % 2, :]
                    nc.tensor.matmul(o, y_hi[:, cols], vh, start=True, stop=False)
                    nc.tensor.matmul(o[:, 0:D], y_hi[:, cols], vl, start=False, stop=False)
                    ins = nc.tensor.matmul(o, y_lo[:, cols], vh, start=False, stop=True)
                ins.then_inc(o_done, 1)

            QPB = H // 4

            def slot(i, k, j, lo, hi):
                head = (i % QPB) * 4 + j
                pair = 2 * i + (j // 2 + 2)
                nxt = i + 1
                pj_head = (nxt % QPB) * 4 + j
                if lo >= -1 and hi + 1 < NH:
                    pe.wait_ge(m_ready, k + 2)
                    if hi + 2 < NH:
                        pe.wait_ge(max_red, 2 * k + 5)
                    else:
                        pe.wait_ge(exp_done, 2 * k + 1)
                    scores(k + 1, (j + 1) % 4, 0)
                if lo >= 0:
                    pe.wait_ge(plo_done, 2 * k + 1)
                    if lo >= 1:
                        pe.wait_ge(yl_ready, k)
                    weigh(j % 2, 0, i // QPB)
                if lo >= -2 and hi + 2 < NH:
                    pe.wait_ge(max_red, 2 * k + 6)
                    if lo >= -2:
                        pe.wait_ge(kl_ready, pairs_so_far(i, j, k))
                    turn_max(k + 2, j % 2)
                if lo >= -1 and hi + 1 < NH:
                    if hi + 2 < NH:
                        pe.wait_ge(max_red, 2 * k + 6)
                    else:
                        pe.wait_ge(exp_done, 2 * k + 2)
                    scores(k + 1, (j + 1) % 4, 1)
                if lo >= 0:
                    pe.wait_ge(plo_done, 2 * k + 2)
                    weigh(j % 2, 1, i // QPB)
                if j % 2 == 0 and hi + 4 < NH:
                    if lo >= -2:
                        pe.wait_ge(m_ready, k + 3)
                    project(0, pair, pj_head * R, nxt // QPB, q_proj)
                if lo >= -3 and hi + 3 < NH:
                    pe.wait_ge(q_spread, 96 * spread_pairs(i, j))
                    pe.wait_ge(k_spread, 96 * spread_pairs(i, j))
                    if lo >= -1:
                        pe.wait_ge(exp_done, 2 * k + 3)
                    if lo + 2 >= 0:
                        pe.wait_ge(max_red, 2 * k + 5)
                    maxima(k + 3, (j + 3) % 4, 0)
                if j % 2 == 0 and hi + 4 < NH:
                    pe.wait_ge(ql_ready, pair + 1)
                    project(1, pair, pj_head * R, nxt // QPB, k_proj)
                if lo >= -3 and hi + 3 < NH:
                    if lo >= -1:
                        pe.wait_ge(exp_done, 2 * k + 4)
                    if lo + 2 >= 0:
                        pe.wait_ge(max_red, 2 * k + 6)
                    maxima(k + 3, (j + 3) % 4, 1)
                if lo >= 0:
                    pe.wait_ge(yl_ready, k + 1)
                    if lo >= 1:
                        pe.wait_ge(o_added, k)
                    outputs(head)

            def pairs_so_far(i, j, k):
                n = 2 * i + (j + 1) // 2 + 2
                return n if not isinstance(n, int) else min(n, NH // 2)

            def spread_pairs(i, j):
                return 2 * i + ((j + 3) // 2 + 1)

            for k in range(-4, 4):
                slot(k // 4, k, k % 4, k, k)
            with pe.Fori(1, NH // 4 - 1) as i:
                for j in range(4):
                    slot(i, 4 * i + j, j, 4 + j, NH - 8 + j)
            for k in range(NH - 4, NH):
                slot(k // 4, k, k % 4, k, k)
            pe.wait_ge(o_added, NH)

            ffn(1)


def kernel(**inputs):
    import numpy as np
    import concourse.bacc as bacc
    from concourse.bass_utils import run_bass_kernel_spmd

    a = {n: np.asarray(v) for n, v in inputs.items()}
    D = a["L0_attn_x"].shape[2]
    arrays = {
        "x": a["L0_attn_x"],
        "wq": a["L0_attn_Q"].transpose(2, 0, 1).reshape(D, -1),
        "wk": a["L0_attn_K"].transpose(2, 0, 1).reshape(D, -1),
        "wvo": a["L0_attn_VO"],
        "qweights": a["L0_ffn_qweights"].transpose(2, 0, 1),
        "scales": a["L0_ffn_scales"].transpose(2, 0, 1),
        "biases": a["L0_ffn_biases"].T,
        "lora_a": a["L0_ffn_lora_a"].transpose(1, 0, 2),
        "lora_b": a["L0_ffn_lora_b"].transpose(2, 0, 1),
        "ln_gamma": a["L0_ffn_ln_gamma"].T,
        "ln_beta": a["L0_ffn_ln_beta"].T,
    }
    arrays = {n: np.ascontiguousarray(v) for n, v in arrays.items()}
    nc = bacc.Bacc("TRN2", target_bir_lowering=False, num_devices=1)
    args = [nc.dram_tensor(n + "_dram", v.shape, mybir.dt.from_np(v.dtype), kind="ExternalInput").ap()
            for n, v in arrays.items()]
    out = nc.dram_tensor("out", a["L0_attn_x"].shape, F32, kind="ExternalOutput").ap()
    macaron(nc, *args, out)
    r = run_bass_kernel_spmd(nc, [{n + "_dram": v for n, v in arrays.items()}], core_ids=[0])
    return r.results[0]["out"]
```

```python
import concourse.bass as bass
from concourse import mybir
from contextlib import ExitStack

F32 = mybir.dt.float32
F16 = mybir.dt.float16
I32 = mybir.dt.int32
ALU = mybir.AluOpType
ACT = mybir.ActivationFunctionType
AX = mybir.AxisListType
RMAX = bass.bass_isa.ReduceOp.max


def macaron(nc, x_d, q_d, k_d, vo_d, qw_d, sc_d, bias_d, la_d, lb_d, gam_d, bet_d, out_d):
    B, T, D = x_d.shape
    H = vo_d.shape[0]
    R = q_d.shape[1] // H
    NL = qw_d.shape[1]
    NB = NL // 2
    G = sc_d.shape[0]
    LR = la_d.shape[0]
    TT = T // 128
    NT = B * TT
    SG = B // 2
    GT = SG * TT
    NH = B * H
    RW = D + 1
    LN_EPS = 1e-5
    MAGIC = float(0x5F3759DF)
    EXPONENT = 0x7F800000
    ONE_BITS2 = float(254 << 23)
    QK_TOP = 2.0 ** -4
    VO_CLAMP = 2.0 ** 14

    ctx = ExitStack()
    with ctx:
        def sb(name, shape, dt=F32):
            return ctx.enter_context(nc.sbuf_tensor(name, shape, dt))

        def sem(name):
            return ctx.enter_context(nc.semaphore(name))

        x = sb("x", [128, NT, D])
        ident = sb("ident", [128, 128])
        ident16 = sb("ident16", [128, 128], F16)
        mean_mat = sb("mean_mat", [128, 128])
        ones_col = sb("ones_col", [128, 1])
        qw = sb("qw", [128, NL, D], I32)
        scl = sb("scl", [128, NL, D])
        la = sb("la", [LR, NL, D])
        lb = sb("lb", [LR, NL, D])
        wt = sb("wt", [128, NL, D])
        wmean = sb("wmean", [128, NL])
        bias = sb("bias", [128, NL])
        bias_c = sb("bias_c", [128, NL])
        gam = sb("gam", [128, NB])
        bet = sb("bet", [128, NB])

        qk32 = sb("qk32", [128, 2, H * R])
        vo32 = sb("vo32", [128, H, D])
        vo_last = sb("vo_last", [128, H, D])
        w_hi = sb("w_hi", [128, 2, H * R], F16)
        w_lo = sb("w_lo", [128, 2, H * R], F16)
        vo_hi = sb("vo_hi", [128, H, RW + 1], F16)
        vo_lo = sb("vo_lo", [128, H, D], F16)
        amax = sb("amax", [128, 4])
        pow2 = sb("pow2", [128, 4])
        inv2 = sb("inv2", [128, 4])
        exp_scale = sb("exp_scale", [128, 1])

        xn_hi = sb("xn_hi", [128, NT, D], F16)
        xn_lo = sb("xn_lo", [128, NT, D], F16)
        xt_hi = sb("xt_hi", [128, B, T], F16)
        xt_lo = sb("xt_lo", [128, B, T], F16)

        stats = sb("stats", [128, GT, 6])
        mv = sb("mv", [128, 2, GT, 2])
        var = sb("var", [128, GT])
        rs_t = sb("rs_t", [128, GT])
        rs_u = sb("rs_u", [128, GT])
        rstd = sb("rstd", [128, 2, GT])
        hT = sb("hT", [128, B, T])
        work_a = sb("work_a", [128, B, T])
        work_b = sb("work_b", [128, B, T])
        xhat = work_a[:, :, :].rearrange("p b (t d) -> p (b t) d", d=D)

        pair_ops = sb("pair_ops", [128, 4, T], F16)
        RING = 4
        head_ops = sb("head_ops", [128, RING, 4, T], F16)
        q1 = head_ops[:, :, 0, :]
        q2 = head_ops[:, :, 1, :]
        k1 = head_ops[:, :, 2, :]
        k2 = head_ops[:, :, 3, :]
        mcol = sb("mcol", [128, 2, TT, 128], F16)
        p32 = work_b[:, :, :].rearrange("p (a t) n -> p a t n", a=2)
        p_hi = sb("p_hi", [128, 2, TT, T], F16)
        p_lo = sb("p_lo", [128, 2, TT, T], F16)
        y_hi = sb("y_hi", [128, T], F16)
        y_lo = sb("y_lo", [128, T], F16)
        rinv = sb("rinv", [128, TT])

        ps = ctx.enter_context(nc.psum_tensor("ps", [128, 8, 512], F32))
        bank = [ps[:, b, :] for b in range(B)]
        s_ps = [ps[:, 2 * a:2 * a + 2, :] for a in range(2)]
        y_ps = ps[:, 4, :]
        qj_ps = ps[:, 5, :]
        kj_ps = ps[:, 7, :]
        o_ps = ps[:, 6:8, 0:2 * RW].rearrange("p b (t n) -> p b t n", n=RW)

        vch = sem("vch")
        s_done = sem("s_done")
        x_in = [sem(f"x_in{b}") for b in range(B)]
        w_in = sem("w_in")
        sc_in = sem("sc_in")
        a_in = sem("a_in")
        consts = sem("consts")
        prep_pe = sem("prep_pe")
        prep_v = sem("prep_v")
        prep_a = sem("prep_a")
        prep_p = sem("prep_p")
        xhat_ready = sem("xhat_ready")
        pre_t = sem("pre_t")
        h_ready = sem("h_ready")
        lin1_done = sem("lin1_done")
        yc_ready = sem("yc_ready")
        sq_ready = sem("sq_ready")
        var_done = sem("var_done")
        rstd_ready = sem("rstd_ready")
        rb_done = sem("rb_done")
        z_ready = sem("z_ready")
        gl_ready = sem("gl_ready")
        lin2_done = sem("lin2_done")
        post_t = sem("post_t")
        x1_ready = sem("x1_ready")
        xn_ready = sem("xn_ready")
        xnl_ready = sem("xnl_ready")
        xn_t = sem("xn_t")
        xnh_ready = sem("xnh_ready")
        xth_ready = sem("xth_ready")
        xsplit_done = sem("xsplit_done")
        out_sem = sem("out_sem")

        q_proj = sem("q_proj")
        k_proj = sem("k_proj")
        qh_ready = sem("qh_ready")
        ql_ready = sem("ql_ready")
        kh_ready = sem("kh_ready")
        kl_ready = sem("kl_ready")
        q_spread = sem("q_spread")
        k_spread = sem("k_spread")
        max_mm = sem("max_mm")
        max_red = sem("max_red")
        m_turned = sem("m_turned")
        m_ready = sem("m_ready")
        exp_done = sem("exp_done")
        phi_done = sem("phi_done")
        plo_done = sem("plo_done")
        av_half = sem("av_half")
        yh_ready = sem("yh_ready")
        yl_ready = sem("yl_ready")
        o_done = sem("o_done")
        o_added = sem("o_added")

        block = ctx.enter_context(nc.Block())

        class Link:
            def __init__(self):
                self.base, self.n = 0, 0

            def __call__(self, eng, ins, alone=False):
                self.n += 1
                ins.then_inc(vch, 1)
                if alone:
                    value = eng.to_reg(self.base + self.n)
                    eng.wait_ge(w_in, 16)
                    eng.wait_ge(vch, value)
                else:
                    eng.wait_ge(vch, self.base + self.n)

        @block.sync
        def _(sp):
            xv = x_d.rearrange("b (n p) d -> p (b n) d", p=128)
            def load_x(b):
                sp.dma_start(x[:, b * TT:(b + 1) * TT, :], xv[:, b * TT:(b + 1) * TT, :]).then_inc(x_in[b], 16)
            load_x(0)
            load_x(1)
            sp.dma_start(qw[:, :, :], qw_d).then_inc(w_in, 16)
            sp.dma_start(la[:, :, :], la_d).then_inc(w_in, 16)
            sp.dma_start(lb[:, :, :], lb_d).then_inc(w_in, 16)
            sp.dma_start(bias[:, :], bias_d).then_inc(w_in, 16)
            sp.dma_start(gam[:, :], gam_d).then_inc(w_in, 16)
            sp.dma_start(bet[:, :], bet_d).then_inc(w_in, 16)
            for b in range(2, B):
                load_x(b)
            sp.dma_start(qk32[:, 0, :], q_d).then_inc(a_in, 16)
            sp.dma_start(qk32[:, 1, :], k_d).then_inc(a_in, 16)
            sp.dma_start(vo32[:, :, :], vo_d.rearrange("h d e -> d h e")).then_inc(a_in, 16)
            sp.dma_start(vo_last[:, :, :], vo_d[:, D - 1, :].partition_broadcast(128)).then_inc(a_in, 16)

            def spread(ready, ring):
                sp.wait_ge(qh_ready, ready)
                sp.wait_ge(ql_ready, ready)
                for e in range(2):
                    half = slice(64 * e, 64 * e + 64)
                    sp.dma_start(head_ops[0:64, ring + e, 0:2, :], pair_ops[half, 0:2, :]).then_inc(q_spread, 16)
                    sp.dma_start(head_ops[64:128, ring + e, 0, :], pair_ops[half, 0, :]).then_inc(q_spread, 16)
                sp.wait_ge(kh_ready, ready)
                sp.wait_ge(kl_ready, ready)
                for e in range(2):
                    half = slice(64 * e, 64 * e + 64)
                    sp.dma_start(head_ops[0:64, ring + e, 2:4, :],
                                 pair_ops[half, 2:3, :].to_broadcast([64, 2, T])).then_inc(k_spread, 16)
                    sp.dma_start(head_ops[64:128, ring + e, 2, :], pair_ops[half, 3, :]).then_inc(k_spread, 16)

            sp.wait_ge(prep_p, 8)
            spread(1, 0)
            spread(2, 2)
            with sp.Fori(0, NH // 4 - 1) as i:
                used = [sp.to_reg(8 * i + 4 * (j + 1)) for j in range(2)]
                ready = [sp.to_reg(2 * i + (j + 3)) for j in range(2)]
                for j in range(2):
                    sp.wait_ge(s_done, used[j])
                    spread(ready[j], 2 * j)

            ov = out_d.rearrange("b (n p) d -> p (b n) d", p=128)
            for b in range(B):
                sp.wait_ge(x1_ready, B + b + 1)
                sp.dma_start(ov[:, b * TT:(b + 1) * TT, :], x[:, b * TT:(b + 1) * TT, :]).then_inc(out_sem, 16)
            sp.wait_ge(out_sem, 16 * B)

        @block.gpsimd
        def _(pool):
            pool.memset(ident[:, :], 0.0).then_inc(prep_p, 1)
            pool.memset(mean_mat[:, :], 1.0 / D).then_inc(consts, 1)
            pool.memset(ones_col[:, :], 1.0 / D).then_inc(consts, 1)
            pool.wait_ge(prep_p, 1)
            pool.affine_select(out=ident[:, :], in_=ident[:, :], compare_op=ALU.not_equal, fill=1.0,
                               base=0, pattern=[[-1, 128]], channel_multiplier=1).then_inc(consts, 1)
            pool.wait_ge(a_in, 16 * 4)
            pool.tensor_tensor(vo32[:, :, :], vo32[:, :, :], vo_last[:, :, :], ALU.subtract).then_inc(prep_p, 1)
            pool.memset(xn_hi[:, :, D - 1:D], 1.0).then_inc(prep_p, 1)
            pool.memset(xn_lo[:, :, D - 1:D], 0.0).then_inc(prep_p, 1)
            pool.memset(mcol[:, :, :, :], 0.0).then_inc(prep_p, 1)
            pool.wait_ge(prep_p, 5)
            pool.memset(head_ops[64:128, :, 1, :], 0.0).then_inc(prep_p, 1)
            pool.wait_ge(prep_p, 6)
            pool.memset(head_ops[64:128, :, 3, :], 0.0).then_inc(prep_p, 1)
            pool.wait_ge(prep_p, 7)
            pool.memset(head_ops[64:65, :, 3, :], 1.0).then_inc(prep_p, 1)
            pool.wait_ge(prep_v, 2)
            pool.wait_ge(prep_p, 8)
            pool.partition_all_reduce(pow2[:, 0:3], amax[:, 0:3], 128, RMAX).then_inc(prep_p, 1)
            pool.wait_ge(prep_a, 3)
            pool.wait_ge(prep_p, 9)
            pool.tensor_tensor(w_lo[:, :, :], qk32[:, :, :], w_hi[:, :, :], ALU.subtract).then_inc(prep_p, 1)
            pool.wait_ge(prep_a, 5)
            pool.tensor_tensor(vo_lo[:, :, :], vo32[:, :, :], vo_hi[:, :, 0:D], ALU.subtract).then_inc(prep_p, 1)
            for b in range(B):
                tiles = slice(b * TT, (b + 1) * TT)
                pool.wait_ge(xnh_ready, b + 1)
                pool.tensor_tensor(xn_lo[:, tiles, 0:D - 1], xhat[:, tiles, 0:D - 1], xn_hi[:, tiles, 0:D - 1],
                                   ALU.subtract).then_inc(xnl_ready, 1)

            def p_low(k, par, a):
                pool.wait_ge(phi_done, 2 * k + (a + 1))
                rows = slice(2 * a, 2 * a + 2)
                pool.tensor_tensor(p_lo[:, par, rows, :], p32[:, par, rows, :], p_hi[:, par, rows, :],
                                   ALU.subtract).then_inc(plo_done, 1)

            for a in range(2):
                p_low(0, 0, a)
            for a in range(2):
                p_low(1, 1, a)
            with pool.Fori(0, NH // 2 - 1) as i:
                for j in range(2):
                    k = 2 * i + (j + 2)
                    for a in range(2):
                        pool.wait_ge(av_half, 2 * (k - 2) + (a + 1))
                        p_low(k, j, a)

        @block.scalar
        def _(act):
            act.dma_start(scl[0:16, :, :], sc_d[0].partition_broadcast(16)).then_inc(sc_in, 16)
            for s in range(1, G):
                act.dma_start(scl[16 * s:16 * s + 16, :, :], sc_d[s].partition_broadcast(16)).then_inc(sc_in, 16)

            act.wait_ge(consts, 3)
            nc.scalar.activation(ident16[:, :], ident[:, :], ACT.Copy).then_inc(prep_a, 1)

            def pre(f, s):
                for c in range(SG):
                    b = s * SG + c
                    act.wait_ge(pre_t, f * B + b + 1)
                    nc.scalar.activation(hT[:, b, :], bank[b], ACT.Copy).then_inc(h_ready, 1)

            def at(f, n, s, c):
                return ((f * NB + n) * 2 + s) * SG + c + 1

            def centre(f, n, s):
                for c in range(SG):
                    b = s * SG + c
                    act.wait_ge(lin1_done, at(f, n, s, c))
                    nc.scalar.activation(work_a[:, b, :], bank[b], ACT.Identity,
                                         bias=bias_c[:, 2 * n:2 * n + 1]).then_inc(yc_ready, 1)
                    nc.scalar.activation(work_b[:, b, :], bank[b], ACT.Square,
                                         bias=bias_c[:, 2 * n:2 * n + 1]).then_inc(sq_ready, 1)

            def gelu(f, n, s):
                for c in range(SG):
                    b = s * SG + c
                    act.wait_ge(z_ready, at(f, n, s, c))
                    nc.scalar.activation(work_a[:, b, :], work_b[:, b, :], ACT.Gelu, scale=gam[:, n:n + 1],
                                         bias=bet[:, n:n + 1]).then_inc(gl_ready, 1)

            def weight_halves():
                act.wait_ge(prep_v, 3)
                for n in range(2):
                    nc.scalar.activation(w_hi[:, n, :], qk32[:, n, :], ACT.Identity, scale=inv2[:, n:n + 1])
                ins = nc.scalar.activation(vo_hi[:, :, 0:D], vo32[:, :, :], ACT.Identity, scale=inv2[:, 2:3])
                ins.then_inc(prep_a, 1)
                act.wait_ge(prep_a, 2)
                for n in range(2):
                    ins = nc.scalar.activation(qk32[:, n, :], qk32[:, n, :], ACT.Identity, scale=inv2[:, n:n + 1])
                ins.then_inc(prep_a, 1)
                nc.scalar.activation(vo_hi[:, :, D:D + 1].rearrange("p h a -> p (h a)"),
                                     ident[:, D - 1:D].to_broadcast([128, H]), ACT.Identity,
                                     scale=inv2[:, 2:3]).then_inc(prep_a, 1)
                nc.scalar.activation(vo32[:, :, :], vo32[:, :, :], ACT.Identity, scale=inv2[:, 2:3]).then_inc(prep_a, 1)

            def split(s):
                for c in range(SG):
                    b = s * SG + c
                    tiles = slice(b * TT, (b + 1) * TT)
                    act.wait_ge(xn_ready, b + 1)
                    nc.scalar.activation(xn_hi[:, tiles, 0:D - 1], xhat[:, tiles, 0:D - 1],
                                         ACT.Copy).then_inc(xnh_ready, 1)
                    act.wait_ge(xn_t, b + 1)
                    nc.scalar.activation(xt_hi[:, b, :], bank[b], ACT.Copy).then_inc(xth_ready, 1)

            def ffn(f):
                pre(f, 0)
                if f == 0:
                    act.wait_ge(prep_v, 1)
                for n in range(NB):
                    centre(f, n, 0)
                    if n:
                        gelu(f, n - 1, 1)
                    else:
                        pre(f, 1)
                    gelu(f, n, 0)
                    centre(f, n, 1)
                    if f == 0 and n == 1:
                        weight_halves()
                gelu(f, NB - 1, 1)
                if f == 0:
                    split(0)
                    split(1)

            ffn(0)

            def q_high(pair):
                act.wait_ge(q_proj, pair + 1)
                nc.scalar.activation(pair_ops[:, 0, :], qj_ps, ACT.Copy).then_inc(qh_ready, 1)

            def k_high(pair):
                act.wait_ge(k_proj, pair + 1)
                nc.scalar.activation(pair_ops[:, 2, :], kj_ps, ACT.Copy).then_inc(kh_ready, 1)

            def row_max(k, ring):
                act.wait_ge(m_turned, k + 1)
                nc.scalar.activation(q2[64:128, ring, :], qj_ps[64:128, :], ACT.Copy).then_inc(m_ready, 1)

            def exps(k, par, a):
                act.wait_ge(s_done, 2 * k + (a + 1))
                nc.scalar.activation(p32[:, par, 2 * a:2 * a + 2, :], s_ps[a], ACT.Exp,
                                     scale=exp_scale[:, 0:1]).then_inc(exp_done, 1)

            def p_high(k, par, a):
                act.wait_ge(exp_done, 2 * k + (a + 1))
                nc.scalar.activation(p_hi[:, par, 2 * a:2 * a + 2, :], p32[:, par, 2 * a:2 * a + 2, :],
                                     ACT.Copy).then_inc(phi_done, 1)

            def y_high(k):
                act.wait_ge(av_half, 2 * k + 2)
                nc.scalar.activation(y_hi[:, :], y_ps, ACT.Copy).then_inc(yh_ready, 1)

            def spread_over(pair):
                act.wait_ge(q_spread, 64 * pair)
                act.wait_ge(k_spread, 64 * pair)

            def slot(k, j, lo, hi):
                if lo >= -1 and hi + 1 < NH:
                    if lo + 1 >= 2:
                        act.wait_ge(plo_done, 2 * (k - 1) + 1)
                        act.wait_ge(av_half, 2 * (k - 1) + 1)
                    exps(k + 1, (j + 1) % 2, 0)
                    p_high(k + 1, (j + 1) % 2, 0)
                if lo >= -2 and hi + 2 < NH:
                    row_max(k + 2, (j + 2) % 4)
                if lo >= -1 and hi + 1 < NH:
                    if lo + 1 >= 2:
                        act.wait_ge(plo_done, 2 * (k - 1) + 2)
                        act.wait_ge(av_half, 2 * (k - 1) + 2)
                    exps(k + 1, (j + 1) % 2, 1)
                if j % 2 == 0 and hi + 4 < NH:
                    pair = (k + 4) // 2 if isinstance(k, int) else pair_of(k, j)
                    if lo > -4:
                        spread_over(pair)
                    q_high(pair)
                    k_high(pair)
                if lo >= 0:
                    if lo >= 1:
                        act.wait_ge(o_done, k)
                    y_high(k)
                if lo >= -1 and hi + 1 < NH:
                    p_high(k + 1, (j + 1) % 2, 1)

            quad = [None]

            def pair_of(k, j):
                return 2 * quad[0] + (j // 2 + 2)

            for k in range(-4, 0):
                slot(k, k % 4, k, k)
            for k in range(0, 4):
                slot(k, k % 4, k, k)
            with act.Fori(1, NH // 4 - 1) as i:
                quad[0] = i
                for j in range(4):
                    slot(4 * i + j, j, 4 + j, NH - 8 + j)
            for k in range(NH - 4, NH):
                slot(k, k % 4, k, k)

            ffn(1)

        @block.vector
        def _(dve):
            link = Link()

            def rsqrt(src, y):
                link(dve, nc.vector.tensor_scalar(var[:, :], src, LN_EPS, None, ALU.add))
                link(dve, nc.vector.tensor_scalar(y.bitcast(I32), var[:, :].bitcast(I32), -0.5, MAGIC,
                                                  ALU.mult, ALU.add))
                for step in range(4):
                    link(dve, nc.vector.scalar_tensor_tensor(rs_t[:, :], y, -0.5, y, ALU.mult, ALU.mult))
                    link(dve, nc.vector.tensor_tensor(rs_u[:, :], rs_t[:, :], var[:, :], ALU.mult))
                    last = nc.vector.scalar_tensor_tensor(y, rs_u[:, :], 1.5, y, ALU.add, ALU.mult)
                    if step < 3:
                        link(dve, last)
                return last

            def weight_maxima():
                dve.wait_ge(a_in, 16 * 4)
                nc.vector.tensor_reduce(amax[:, 0:1], qk32[:, 0, :], AX.X, ALU.max, apply_absolute_value=True)
                nc.vector.tensor_reduce(amax[:, 1:2], qk32[:, 1, :], AX.X, ALU.max, apply_absolute_value=True)
                dve.wait_ge(prep_p, 2)
                link(dve, nc.vector.tensor_reduce(amax[:, 2:3], vo32[:, :, :].rearrange("p h d -> p (h d)"), AX.X,
                                                  ALU.max, apply_absolute_value=True))
                nc.vector.tensor_scalar(amax[:, 0:3], amax[:, 0:3], 1e-30, None, ALU.max).then_inc(prep_v, 1)

            def weight_scales():
                dve.wait_ge(prep_p, 9)
                link(dve, nc.vector.tensor_scalar(pow2[:, 0:3].bitcast(I32), pow2[:, 0:3].bitcast(I32), EXPONENT,
                                                  None, ALU.bitwise_and))
                link(dve, nc.vector.tensor_scalar(inv2[:, 0:3].bitcast(I32), pow2[:, 0:3].bitcast(I32), -1.0,
                                                  ONE_BITS2, ALU.mult, ALU.add))
                link(dve, nc.vector.tensor_scalar(inv2[:, 0:2], inv2[:, 0:2], QK_TOP, None, ALU.mult))
                link(dve, nc.vector.tensor_scalar(inv2[:, 2:3], inv2[:, 2:3], VO_CLAMP, 1.0 / VO_CLAMP,
                                                  ALU.min, ALU.max))
                nc.vector.tensor_scalar(exp_scale[:, :], pow2[:, 0:1], pow2[:, 1:2],
                                        1.0 / (QK_TOP * QK_TOP * float(D) ** 0.5), ALU.mult,
                                        ALU.mult).then_inc(prep_v, 1)

            def norm_tokens(f, s, ready, loaded):
                for c in range(SG):
                    if loaded:
                        dve.wait_ge(x_in[s * SG + c], 16)
                    for t in range(c * TT, (c + 1) * TT):
                        ins = nc.vector.bn_stats(stats[:, t, :], x[:, s * GT + t, :])
                link(dve, ins)
                for t in range(GT):
                    ins = nc.vector.bn_aggr(mv[:, s, t, :], stats[:, t, :])
                link(dve, ins)
                link(dve, rsqrt(mv[:, s, :, 1], rstd[:, s, :]))
                for c in range(SG):
                    for t in range(c * TT, (c + 1) * TT):
                        ins = nc.vector.tensor_scalar(xhat[:, s * GT + t, :], x[:, s * GT + t, :], mv[:, s, t, 0:1],
                                                      rstd[:, s, t:t + 1], ALU.subtract, ALU.mult)
                    ins.then_inc(ready, 1)

            norm_tokens(0, 0, xhat_ready, True)

            dve.wait_ge(w_in, 16 * 6)
            link(dve, nc.vector.tensor_scalar(wt[:, :, :], qw[:, :, :], 1.0 / 7.5, -1.0, ALU.mult, ALU.add))
            dve.wait_ge(sc_in, 16 * G)
            link(dve, nc.vector.tensor_tensor(wt[:, :, :], wt[:, :, :], scl[:, :, :], ALU.mult))
            dve.wait_ge(prep_pe, 1)
            for b in range(2):
                half = slice(3 * b, 3 * b + 3)
                ins = nc.vector.tensor_tensor(
                    wt[:, half, :], ps[:, SG + b, 0:3 * D].rearrange("p (n d) -> p n d", n=3), wt[:, half, :], ALU.add)
                link(dve, ins)
            link(dve, nc.vector.tensor_reduce(wmean[:, :], wt[:, :, :], AX.X, ALU.add))
            link(dve, nc.vector.tensor_scalar(wmean[:, :], wmean[:, :], -1.0 / D, None, ALU.mult))
            for n in range(0, NL, 2):
                link(dve, nc.vector.tensor_scalar(wt[:, n, :], wt[:, n, :], wmean[:, n:n + 1], None, ALU.add))
            link(dve, nc.vector.tensor_copy(bias_c[:, :], bias[:, :]))
            nc.vector.tensor_tensor(bias_c[:, 0:NL:2], bias[:, 0:NL:2], ps[:, SG + 2, 0:NL:2],
                                    ALU.subtract).then_inc(prep_v, 1)

            def at(f, n, s, c):
                return ((f * NB + n) * 2 + s) * SG + c + 1

            def step_rsqrt(f, n, s):
                dve.wait_ge(var_done, at(f, n, s, SG - 1))
                rsqrt(bank[s * SG][:, 0:GT], rstd[:, s, :]).then_inc(rstd_ready, 1)

            def step_z(f, n, s):
                for c in range(SG):
                    b = s * SG + c
                    dve.wait_ge(yc_ready, at(f, n, s, c))
                    dve.wait_ge(rb_done, at(f, n, s, c))
                    nc.vector.tensor_tensor(work_b[:, b, :], bank[b], work_a[:, b, :],
                                            ALU.mult).then_inc(z_ready, 1)

            def step_h(f, n, s):
                for c in range(SG):
                    b = s * SG + c
                    dve.wait_ge(lin2_done, at(f, n, s, c))
                    nc.vector.scalar_tensor_tensor(hT[:, b, :], bank[b], bias[:, 2 * n + 1:2 * n + 2], hT[:, b, :],
                                                   ALU.add, ALU.add).then_inc(h_ready, 1)

            def step_x(f, s):
                for c in range(SG):
                    b = s * SG + c
                    dve.wait_ge(post_t, f * B + b + 1)
                    rows = x[:, b * TT:(b + 1) * TT, :].rearrange("p a d -> p (a d)")
                    ins = nc.vector.scalar_tensor_tensor(rows, bank[b], 0.5, rows, ALU.mult, ALU.add)
                    ins.then_inc(x1_ready, 1)

            def split(s):
                for c in range(SG):
                    b = s * SG + c
                    dve.wait_ge(xth_ready, b + 1)
                    nc.vector.tensor_tensor(xt_lo[:, b, :], bank[b], xt_hi[:, b, :],
                                            ALU.subtract).then_inc(xsplit_done, 1)

            def ffn(f):
                if f:
                    norm_tokens(f, 0, xhat_ready, False)
                norm_tokens(f, 1, xhat_ready, f == 0)
                for n in range(NB):
                    if n:
                        step_z(f, n - 1, 1)
                    step_rsqrt(f, n, 0)
                    if n:
                        step_h(f, n - 1, 1)
                    step_z(f, n, 0)
                    if f == 0 and n == 0:
                        weight_maxima()
                    step_h(f, n, 0)
                    if f == 0 and n == 0:
                        weight_scales()
                    step_rsqrt(f, n, 1)
                step_x(f, 0)
                step_z(f, NB - 1, 1)
                if f == 0:
                    dve.wait_ge(x1_ready, SG)
                    norm_tokens(f, 0, xn_ready, False)
                step_h(f, NB - 1, 1)
                step_x(f, 1)
                if f == 0:
                    split(0)
                    dve.wait_ge(x1_ready, B)
                    norm_tokens(f, 1, xn_ready, False)
                    split(1)

            ffn(0)

            ADD_LINKS = 1

            def q_low(pair):
                dve.wait_ge(qh_ready, pair + 1)
                nc.vector.tensor_tensor(pair_ops[:, 1, :], qj_ps, pair_ops[:, 0, :], ALU.subtract).then_inc(ql_ready, 1)

            def k_low(pair):
                dve.wait_ge(kh_ready, pair + 1)
                nc.vector.tensor_tensor(pair_ops[:, 3, :], kj_ps, pair_ops[:, 2, :], ALU.subtract).then_inc(kl_ready, 1)

            def reduce_max(k, par, a):
                dve.wait_ge(max_mm, 2 * k + (a + 1))
                nc.vector.tensor_reduce(mcol[:, par, 2 * a:2 * a + 2, R], s_ps[a], AX.X, ALU.max,
                                        negate=True).then_inc(max_red, 1)

            def y_low(k):
                dve.wait_ge(yh_ready, k + 1)
                nc.vector.tensor_tensor(y_lo[:, :], y_ps, y_hi[:, :], ALU.subtract).then_inc(yl_ready, 1)

            def add_out(mine, k, batch):
                dve.wait_ge(o_done, k + 1)
                mine(dve, nc.vector.reciprocal(rinv[:, :].rearrange("p (a b) -> p a b", a=2), o_ps[:, :, :, D]))
                for t in range(TT):
                    row = x[:, bass.ds(batch * TT + t, 1), :].rearrange("p a d -> p (a d)")
                    ins = nc.vector.scalar_tensor_tensor(row, o_ps[:, t // 2, t % 2, 0:D], rinv[:, t:t + 1], row,
                                                         ALU.mult, ALU.add)
                ins.then_inc(o_added, 1)

            def slot(mine, i, k, j, lo, hi):
                if lo >= 1 and lo - 1 < NH:
                    if lo >= 2:
                        dve.wait_ge(o_added, k - 1)
                    add_out(mine, k - 1, (i * 4 + (j - 1)) // H)
                if j % 2 == 0 and lo >= -3 and hi + 3 < NH:
                    maxima(k, j, lo, 0)
                pair = 2 * i + (j // 2 + 2)
                if j % 2 == 0 and hi + 4 < NH:
                    if lo > -4:
                        dve.wait_ge(q_spread, 64 * pair)
                        dve.wait_ge(k_spread, 64 * pair)
                    q_low(pair)
                    k_low(pair)
                if 0 <= lo and hi < NH:
                    y_low(k)
                if lo >= -3 and hi + 3 < NH:
                    if j % 2:
                        maxima(k, j, lo, 0)
                    maxima(k, j, lo, 1)

            def maxima(k, j, lo, a):
                if lo + 3 >= 2 and a == 0:
                    dve.wait_ge(m_turned, k + 2)
                reduce_max(k + 3, (j + 3) % 2, a)

            for k in range(-4, 4):
                slot(link, k // 4, k, k % 4, k, k)
            start = link.base + link.n
            with dve.Fori(1, NH // 4 - 1) as i:
                mine = Link()
                mine.base = i * (4 * ADD_LINKS) + (start - 4 * ADD_LINKS)
                for j in range(4):
                    slot(mine, i, 4 * i + j, j, 4 + j, NH - 8 + j)
            link.base, link.n = start + (NH // 4 - 2) * 4 * ADD_LINKS, 0
            for k in range(NH - 4, NH + 1):
                slot(link, k // 4, k, k % 4, k, k)
            dve.wait_ge(o_added, NH)

            ffn(1)

        @block.tensor
        def _(pe):
            pe.wait_ge(w_in, 16 * 6)
            pe.wait_ge(consts, 3)
            nc.tensor.matmul(ps[:, SG + 2, 0:NL], mean_mat[:, :], bias[:, :], start=True, stop=True)
            for n in range(NL):
                ins = nc.tensor.matmul(ps[:, SG + n // 3, (n % 3) * D:(n % 3 + 1) * D], la[:, n, :], lb[:, n, :],
                                       start=True, stop=True)
            ins.then_inc(prep_pe, 1)

            def turn(b, src, done):
                for t in range(TT):
                    ins = nc.tensor.transpose(bank[b][:, t * 128:(t + 1) * 128], src(t), ident[:, :])
                ins.then_inc(done, 1)

            def at(f, n, s, c):
                return ((f * NB + n) * 2 + s) * SG + c + 1

            def batches(s):
                return [(c, s * SG + c) for c in range(SG)]

            def pre(f, s):
                for c, b in batches(s):
                    pe.wait_ge(xhat_ready, f * B + b + 1)
                    turn(b, lambda t: xhat[:, b * TT + t, :], pre_t)

            def lin1(f, n, s):
                for c, b in batches(s):
                    pe.wait_ge(h_ready, f * (NB + 1) * B + (b + 1 if n == 0 else B + ((n - 1) * 2 + s) * SG + c + 1))
                    nc.tensor.matmul(bank[b], wt[:, 2 * n, :], hT[:, b, :], start=True, stop=True).then_inc(lin1_done, 1)

            def variance(f, n, s):
                for c, b in batches(s):
                    pe.wait_ge(sq_ready, at(f, n, s, c))
                    for t in range(TT):
                        col = c * TT + t
                        ins = nc.tensor.matmul(bank[s * SG][:, col:col + 1], work_b[:, b, t * 128:(t + 1) * 128],
                                               ones_col[:, :], start=True, stop=True)
                    ins.then_inc(var_done, 1)

            def spread_rstd(f, n, s):
                pe.wait_ge(rstd_ready, (f * NB + n) * 2 + s + 1)
                for c, b in batches(s):
                    for t in range(TT):
                        col = c * TT + t
                        ins = nc.tensor.matmul(bank[b][:, t * 128:(t + 1) * 128],
                                               rstd[:, s, col:col + 1].to_broadcast([128, 128]), ident[:, :],
                                               start=True, stop=True)
                    ins.then_inc(rb_done, 1)

            def lin2(f, n, s):
                for c, b in batches(s):
                    pe.wait_ge(gl_ready, at(f, n, s, c))
                    nc.tensor.matmul(bank[b], wt[:, 2 * n + 1, :], work_a[:, b, :], start=True,
                                     stop=True).then_inc(lin2_done, 1)

            def post(f, s):
                for c, b in batches(s):
                    pe.wait_ge(h_ready, f * (NB + 1) * B + B + ((NB - 1) * 2 + s) * SG + c + 1)
                    turn(b, lambda t: hT[:, b, t * 128:(t + 1) * 128], post_t)

            def turn_xn(s):
                for c, b in batches(s):
                    pe.wait_ge(xn_ready, b + 1)
                    turn(b, lambda t: xhat[:, b * TT + t, :], xn_t)

            def ffn(f):
                pre(f, 0)
                if f == 0:
                    pe.wait_ge(prep_v, 1)
                for n in range(NB):
                    lin1(f, n, 0)
                    if n:
                        spread_rstd(f, n - 1, 1)
                    variance(f, n, 0)
                    if n:
                        lin2(f, n - 1, 1)
                    else:
                        pre(f, 1)
                    spread_rstd(f, n, 0)
                    lin1(f, n, 1)
                    lin2(f, n, 0)
                    variance(f, n, 1)
                post(f, 0)
                spread_rstd(f, NB - 1, 1)
                lin2(f, NB - 1, 1)
                if f == 0:
                    turn_xn(0)
                post(f, 1)
                if f == 0:
                    turn_xn(1)

            ffn(0)

            pe.wait_ge(prep_a, 5)
            pe.wait_ge(prep_p, 11)
            pe.wait_ge(xsplit_done, B)
            pe.wait_ge(xnl_ready, B)

            def project(dst, which, pair, col, batch, done):
                hi = w_hi[:, which, bass.ds(col, 128)]
                lo = w_lo[:, which, bass.ds(col, 128)]
                xh = xt_hi[:, bass.ds(batch, 1), :].rearrange("p a t -> p (a t)")
                xl = xt_lo[:, bass.ds(batch, 1), :].rearrange("p a t -> p (a t)")
                nc.tensor.matmul(dst, hi, xh, start=True, stop=False)
                nc.tensor.matmul(dst, hi, xl, start=False, stop=False)
                nc.tensor.matmul(dst, lo, xh, start=False, stop=True).then_inc(done, 1)

            def maxima(k, ring, a):
                for t in (2 * a, 2 * a + 1):
                    ins = nc.tensor.matmul(s_ps[a][:, t % 2, :], q1[:, ring, t * 128:(t + 1) * 128], k1[:, ring, :],
                                           start=True, stop=True)
                ins.then_inc(max_mm, 1)

            def turn_max(k, par):
                for t in range(TT):
                    ins = nc.tensor.matmul(qj_ps[:, t * 128:(t + 1) * 128], mcol[:, par, t, :], ident16[:, :],
                                           start=True, stop=True)
                ins.then_inc(m_turned, 1)

            def scores(k, ring, a):
                for u in (2 * a, 2 * a + 1):
                    keys = slice(u * 128, (u + 1) * 128)
                    nc.tensor.matmul(s_ps[a][:, u % 2, :], k1[:, ring, keys], q1[:, ring, :], start=True, stop=False)
                    ins = nc.tensor.matmul(s_ps[a][:, u % 2, :], k2[:, ring, keys], q2[:, ring, :],
                                           start=False, stop=True)
                ins.then_inc(s_done, 1)

            def weigh(par, a, batch):
                for u in (2 * a, 2 * a + 1):
                    row = bass.ds(batch * TT + u, 1)
                    xh = xn_hi[:, row, :].rearrange("p a d -> p (a d)")
                    xl = xn_lo[:, row, :].rearrange("p a d -> p (a d)")
                    nc.tensor.matmul(y_ps, xh, p_hi[:, par, u, :], start=(u == 0), stop=False)
                    nc.tensor.matmul(y_ps, xl, p_hi[:, par, u, :], start=False, stop=False)
                    ins = nc.tensor.matmul(y_ps, xh, p_lo[:, par, u, :], start=False, stop=(u == TT - 1))
                ins.then_inc(av_half, 1)

            def outputs(head):
                vh = vo_hi[:, bass.ds(head, 1), 0:RW].rearrange("p a d -> p (a d)")
                vl = vo_lo[:, bass.ds(head, 1), :].rearrange("p a d -> p (a d)")
                for t in range(TT):
                    cols = slice(t * 128, (t + 1) * 128)
                    o = o_ps[:, t // 2, t % 2, :]
                    nc.tensor.matmul(o, y_hi[:, cols], vh, start=True, stop=False)
                    nc.tensor.matmul(o[:, 0:D], y_hi[:, cols], vl, start=False, stop=False)
                    ins = nc.tensor.matmul(o, y_lo[:, cols], vh, start=False, stop=True)
                ins.then_inc(o_done, 1)

            QPB = H // 4

            def slot(i, k, j, lo, hi):
                pair = 2 * i + (j // 2 + 2)
                pj_head = ((i + 1) % QPB) * 4 + j
                if lo >= 1:
                    pe.wait_ge(yl_ready, k)
                    if lo >= 2:
                        pe.wait_ge(o_added, k - 1)
                    pe.wait_ge(kl_ready, pairs_so_far(i, j, k))
                    outputs((4 * i + (j - 1)) % H)
                if lo >= -1 and hi + 1 < NH:
                    pe.wait_ge(m_ready, k + 2)
                    if hi + 2 < NH:
                        pe.wait_ge(max_red, 2 * k + 5)
                    else:
                        pe.wait_ge(exp_done, 2 * k + 1)
                    scores(k + 1, (j + 1) % 4, 0)
                if 0 <= lo < NH:
                    pe.wait_ge(plo_done, 2 * k + 1)
                    weigh(j % 2, 0, i // QPB)
                if lo >= -2 and hi + 2 < NH:
                    pe.wait_ge(max_red, 2 * k + 6)
                    pe.wait_ge(ql_ready, pairs_so_far(i, j, k))
                    turn_max(k + 2, j % 2)
                if lo >= -1 and hi + 1 < NH:
                    if hi + 2 < NH:
                        pe.wait_ge(max_red, 2 * k + 6)
                    else:
                        pe.wait_ge(exp_done, 2 * k + 2)
                    scores(k + 1, (j + 1) % 4, 1)
                if j % 2 == 0:
                    first_maxima(i, k, j, lo, hi)
                if j % 2 == 0 and hi + 4 < NH:
                    if lo >= -2:
                        pe.wait_ge(m_ready, k + 3)
                    project(qj_ps, 0, pair, pj_head * R, (i + 1) // QPB, q_proj)
                    if lo >= 1:
                        pe.wait_ge(o_added, k)
                    project(kj_ps, 1, pair, pj_head * R, (i + 1) // QPB, k_proj)
                if 0 <= lo < NH:
                    pe.wait_ge(plo_done, 2 * k + 2)
                    weigh(j % 2, 1, i // QPB)
                if j % 2:
                    first_maxima(i, k, j, lo, hi)
                if lo >= -3 and hi + 3 < NH:
                    if lo >= -1:
                        pe.wait_ge(exp_done, 2 * k + 4)
                    if lo + 2 >= 0:
                        pe.wait_ge(max_red, 2 * k + 6)
                    maxima(k + 3, (j + 3) % 4, 1)

            def first_maxima(i, k, j, lo, hi):
                if lo >= -3 and hi + 3 < NH:
                    pe.wait_ge(q_spread, 64 * spread_pairs(i, j))
                    pe.wait_ge(k_spread, 64 * spread_pairs(i, j))
                    if lo >= -1:
                        pe.wait_ge(exp_done, 2 * k + 3)
                    if lo + 2 >= 0:
                        pe.wait_ge(max_red, 2 * k + 5)
                    maxima(k + 3, (j + 3) % 4, 0)

            def pairs_so_far(i, j, k):
                n = 2 * i + ((j + 3) // 2 + 1)
                return n if not isinstance(n, int) else min(n, NH // 2)

            def spread_pairs(i, j):
                return 2 * i + ((j + 3) // 2 + 1)

            for k in range(-4, 4):
                slot(k // 4, k, k % 4, k, k)
            with pe.Fori(1, NH // 4 - 1) as i:
                for j in range(4):
                    slot(i, 4 * i + j, j, 4 + j, NH - 8 + j)
            for k in range(NH - 4, NH + 1):
                slot(k // 4, k, k % 4, k, k)
            pe.wait_ge(o_added, NH)

            ffn(1)


def kernel(**inputs):
    import numpy as np
    import concourse.bacc as bacc
    from concourse.bass_utils import run_bass_kernel_spmd

    a = {n: np.asarray(v) for n, v in inputs.items()}
    D = a["L0_attn_x"].shape[2]
    arrays = {
        "x": a["L0_attn_x"],
        "wq": a["L0_attn_Q"].transpose(2, 0, 1).reshape(D, -1),
        "wk": a["L0_attn_K"].transpose(2, 0, 1).reshape(D, -1),
        "wvo": a["L0_attn_VO"],
        "qweights": a["L0_ffn_qweights"].transpose(2, 0, 1),
        "scales": a["L0_ffn_scales"].transpose(2, 0, 1),
        "biases": a["L0_ffn_biases"].T,
        "lora_a": a["L0_ffn_lora_a"].transpose(1, 0, 2),
        "lora_b": a["L0_ffn_lora_b"].transpose(2, 0, 1),
        "ln_gamma": a["L0_ffn_ln_gamma"].T,
        "ln_beta": a["L0_ffn_ln_beta"].T,
    }
    arrays = {n: np.ascontiguousarray(v) for n, v in arrays.items()}
    nc = bacc.Bacc("TRN2", target_bir_lowering=False, num_devices=1)
    args = [nc.dram_tensor(n + "_dram", v.shape, mybir.dt.from_np(v.dtype), kind="ExternalInput").ap()
            for n, v in arrays.items()]
    out = nc.dram_tensor("out", a["L0_attn_x"].shape, F32, kind="ExternalOutput").ap()
    macaron(nc, *args, out)
    r = run_bass_kernel_spmd(nc, [{n + "_dram": v for n, v in arrays.items()}], core_ids=[0])
    return r.results[0]["out"]
```

```python
import concourse.bass as bass
from concourse import mybir
from contextlib import ExitStack

F32 = mybir.dt.float32
F16 = mybir.dt.float16
I32 = mybir.dt.int32
ALU = mybir.AluOpType
ACT = mybir.ActivationFunctionType
AX = mybir.AxisListType
RMAX = bass.bass_isa.ReduceOp.max


def macaron(nc, x_d, q_d, k_d, vo_d, qw_d, sc_d, bias_d, la_d, lb_d, gam_d, bet_d, out_d):
    B, T, D = x_d.shape
    H = vo_d.shape[0]
    R = q_d.shape[1] // H
    NL = qw_d.shape[1]
    NB = NL // 2
    G = sc_d.shape[0]
    LR = la_d.shape[0]
    TT = T // 128
    NT = B * TT
    SG = B // 2
    GT = SG * TT
    NH = B * H
    RW = D + 1
    LN_EPS = 1e-5
    MAGIC = float(0x5F3759DF)
    EXPONENT = 0x7F800000
    ONE_BITS2 = float(254 << 23)
    QK_TOP = 2.0 ** -4
    VO_CLAMP = 2.0 ** 14

    ctx = ExitStack()
    with ctx:
        def sb(name, shape, dt=F32):
            return ctx.enter_context(nc.sbuf_tensor(name, shape, dt))

        def sem(name):
            return ctx.enter_context(nc.semaphore(name))

        x = sb("x", [128, NT, D])
        ident = sb("ident", [128, 128])
        ident16 = sb("ident16", [128, 128], F16)
        mean_mat = sb("mean_mat", [128, 128])
        ones_col = sb("ones_col", [128, 1])
        qw = sb("qw", [128, NL, D], I32)
        scl = sb("scl", [128, NL, D])
        la = sb("la", [LR, NL, D])
        lb = sb("lb", [LR, NL, D])
        wt = sb("wt", [128, NL, D])
        wmean = sb("wmean", [128, NL])
        bias = sb("bias", [128, NL])
        bias_c = sb("bias_c", [128, NL])
        gam = sb("gam", [128, NB])
        bet = sb("bet", [128, NB])

        qk32 = sb("qk32", [128, 2, H * R])
        vo32 = sb("vo32", [128, H, D])
        vo_last = sb("vo_last", [128, H, D])
        w_hi = sb("w_hi", [128, 2, H * R], F16)
        w_lo = sb("w_lo", [128, 2, H * R], F16)
        vo_hi = sb("vo_hi", [128, H, RW + 1], F16)
        vo_lo = sb("vo_lo", [128, H, D], F16)
        amax = sb("amax", [128, 4])
        pow2 = sb("pow2", [128, 4])
        inv2 = sb("inv2", [128, 4])
        exp_scale = sb("exp_scale", [128, 1])

        xn_hi = sb("xn_hi", [128, NT, D], F16)
        xn_lo = sb("xn_lo", [128, NT, D], F16)
        xt_hi = sb("xt_hi", [128, B, T], F16)
        xt_lo = sb("xt_lo", [128, B, T], F16)

        stats = sb("stats", [128, GT, 6])
        mv = sb("mv", [128, 2, GT, 2])
        var = sb("var", [128, GT])
        rs_t = sb("rs_t", [128, GT])
        rs_u = sb("rs_u", [128, GT])
        rstd = sb("rstd", [128, 2, GT])
        shift = sb("shift", [128, 2, GT])
        hT = sb("hT", [128, B, T])
        work_a = sb("work_a", [128, B, T])
        work_b = sb("work_b", [128, B, T])
        xhat = work_a[:, :, :].rearrange("p b (t d) -> p (b t) d", d=D)

        pair_ops = sb("pair_ops", [128, 4, T], F16)
        RING = 4
        head_ops = sb("head_ops", [128, RING, 4, T], F16)
        q1 = head_ops[:, :, 0, :]
        q2 = head_ops[:, :, 1, :]
        k1 = head_ops[:, :, 2, :]
        k2 = head_ops[:, :, 3, :]
        mcol = sb("mcol", [128, 2, TT, 128], F16)
        p32 = work_b[:, :, :].rearrange("p (a t) n -> p a t n", a=2)
        p_hi = sb("p_hi", [128, 2, TT, T], F16)
        p_lo = sb("p_lo", [128, 2, TT, T], F16)
        y_hi = sb("y_hi", [128, T], F16)
        y_lo = sb("y_lo", [128, T], F16)
        rinv = sb("rinv", [128, TT])

        ps = ctx.enter_context(nc.psum_tensor("ps", [128, 8, 512], F32))
        bank = [ps[:, b, :] for b in range(B)]
        s_ps = [ps[:, 2 * a:2 * a + 2, :] for a in range(2)]
        y_ps = ps[:, 4, :]
        qj_ps = ps[:, 5, :]
        kj_ps = ps[:, 7, :]
        o_ps = ps[:, 6:8, 0:2 * RW].rearrange("p b (t n) -> p b t n", n=RW)

        vch = sem("vch")
        s_done = sem("s_done")
        x_in = [sem(f"x_in{b}") for b in range(B)]
        w_in = sem("w_in")
        sc_in = sem("sc_in")
        a_in = sem("a_in")
        consts = sem("consts")
        prep_pe = sem("prep_pe")
        prep_v = sem("prep_v")
        prep_a = sem("prep_a")
        prep_p = sem("prep_p")
        moments_ready = sem("moments_ready")
        xhat_v = sem("xhat_v")
        xhat_a = sem("xhat_a")
        pre_t = sem("pre_t")
        h_ready = sem("h_ready")
        lin1_done = sem("lin1_done")
        yc_ready = sem("yc_ready")
        sq_ready = sem("sq_ready")
        var_done = sem("var_done")
        rstd_ready = sem("rstd_ready")
        rb_done = sem("rb_done")
        z_ready = sem("z_ready")
        gl_ready = sem("gl_ready")
        lin2_done = sem("lin2_done")
        post_t = sem("post_t")
        x1_ready = sem("x1_ready")
        xnl_ready = sem("xnl_ready")
        xn_t = sem("xn_t")
        xnh_ready = sem("xnh_ready")
        xth_ready = sem("xth_ready")
        xsplit_done = sem("xsplit_done")
        out_sem = sem("out_sem")

        q_proj = sem("q_proj")
        k_proj = sem("k_proj")
        qh_ready = sem("qh_ready")
        ql_ready = sem("ql_ready")
        kh_ready = sem("kh_ready")
        kl_ready = sem("kl_ready")
        q2_spread = sem("q2_spread")
        spread_done = [sem("spread_even"), sem("spread_odd")]
        max_mm = sem("max_mm")
        max_red = sem("max_red")
        m_turned = sem("m_turned")
        m_ready = sem("m_ready")
        exp_done = sem("exp_done")
        phi_done = sem("phi_done")
        plo_done = sem("plo_done")
        av_half = sem("av_half")
        yh_ready = sem("yh_ready")
        yl_ready = sem("yl_ready")
        o_done = sem("o_done")
        o_added = sem("o_added")

        block = ctx.enter_context(nc.Block())

        def late_turns(k):
            return range(SG + (k + 2) * (SG // 2), SG + (k + 3) * (SG // 2))

        def late_bank(b):
            return ps[:, 4 + 2 * (b % 2), :]

        def wait_xhat(eng, u, c):
            if c < SG // 2:
                eng.wait_ge(xhat_v, u * (SG // 2) + c + 1)
            else:
                eng.wait_ge(xhat_a, (u - 1) * (SG // 2) + c + 1)

        class Link:
            def __init__(self):
                self.base, self.n = 0, 0

            def __call__(self, eng, ins, alone=False):
                self.n += 1
                ins.then_inc(vch, 1)
                if alone:
                    value = eng.to_reg(self.base + self.n)
                    eng.wait_ge(w_in, 16)
                    eng.wait_ge(vch, value)
                else:
                    eng.wait_ge(vch, self.base + self.n)

        @block.sync
        def _(sp):
            xv = x_d.rearrange("b (n p) d -> p (b n) d", p=128)
            def load_x(b):
                sp.dma_start(x[:, b * TT:(b + 1) * TT, :], xv[:, b * TT:(b + 1) * TT, :]).then_inc(x_in[b], 16)
            for b in range(SG):
                load_x(b)
            sp.dma_start(qw[:, :, :], qw_d).then_inc(w_in, 16)
            sp.dma_start(la[:, :, :], la_d).then_inc(w_in, 16)
            sp.dma_start(lb[:, :, :], lb_d).then_inc(w_in, 16)
            sp.dma_start(bias[:, :], bias_d).then_inc(w_in, 16)
            sp.dma_start(gam[:, :], gam_d).then_inc(w_in, 16)
            sp.dma_start(bet[:, :], bet_d).then_inc(w_in, 16)
            for b in range(SG, B):
                load_x(b)
            sp.dma_start(qk32[:, 0, :], q_d).then_inc(a_in, 16)
            sp.dma_start(qk32[:, 1, :], k_d).then_inc(a_in, 16)
            sp.dma_start(vo32[:, :, :], vo_d.rearrange("h d e -> d h e")).then_inc(a_in, 16)
            sp.dma_start(vo_last[:, :, :], vo_d[:, D - 1, :].partition_broadcast(128)).then_inc(a_in, 16)

            def spread(ready, ring):
                def q_halves(e):
                    half = slice(64 * e, 64 * e + 64)
                    sp.dma_start(head_ops[0:64, ring + e, 0, :], pair_ops[half, 0, :]).then_inc(spread_done[e], 16)
                    sp.dma_start(head_ops[64:128, ring + e, 0, :], pair_ops[half, 0, :]).then_inc(spread_done[e], 16)

                def k_halves(e):
                    half = slice(64 * e, 64 * e + 64)
                    sp.dma_start(head_ops[0:64, ring + e, 2:4, :],
                                 pair_ops[half, 2:3, :].to_broadcast([64, 2, T])).then_inc(spread_done[e], 16)

                def lows(e):
                    half = slice(64 * e, 64 * e + 64)
                    sp.dma_start(head_ops[64:128, ring + e, 2, :], pair_ops[half, 3, :]).then_inc(spread_done[e], 16)
                    sp.dma_start(head_ops[0:64, ring + e, 1, :], pair_ops[half, 1, :]).then_inc(q2_spread, 16)

                sp.wait_ge(qh_ready, ready)
                q_halves(0)
                sp.wait_ge(kh_ready, ready)
                k_halves(0)
                sp.wait_ge(ql_ready, ready)
                sp.wait_ge(kl_ready, ready)
                lows(0)
                q_halves(1)
                k_halves(1)
                lows(1)

            sp.wait_ge(prep_p, 8)
            spread(1, 0)
            spread(2, 2)
            with sp.Fori(0, NH // 4 - 1) as i:
                used = [sp.to_reg(8 * i + 4 * (j + 1)) for j in range(2)]
                ready = [sp.to_reg(2 * i + (j + 3)) for j in range(2)]
                for j in range(2):
                    sp.wait_ge(s_done, used[j])
                    spread(ready[j], 2 * j)

            ov = out_d.rearrange("b (n p) d -> p (b n) d", p=128)
            for b in range(B):
                sp.wait_ge(x1_ready, B + b + 1)
                sp.dma_start(ov[:, b * TT:(b + 1) * TT, :], x[:, b * TT:(b + 1) * TT, :]).then_inc(out_sem, 16)
            sp.wait_ge(out_sem, 16 * B)

        @block.gpsimd
        def _(pool):
            pool.memset(ident[:, :], 0.0).then_inc(prep_p, 1)
            pool.memset(mean_mat[:, :], 1.0 / D).then_inc(consts, 1)
            pool.memset(ones_col[:, :], 1.0 / D).then_inc(consts, 1)
            pool.wait_ge(prep_p, 1)
            pool.affine_select(out=ident[:, :], in_=ident[:, :], compare_op=ALU.not_equal, fill=1.0,
                               base=0, pattern=[[-1, 128]], channel_multiplier=1).then_inc(consts, 1)
            pool.wait_ge(a_in, 16 * 4)
            pool.tensor_tensor(vo32[:, :, :], vo32[:, :, :], vo_last[:, :, :], ALU.subtract).then_inc(prep_p, 1)
            pool.memset(xn_hi[:, :, D - 1:D], 1.0).then_inc(prep_p, 1)
            pool.memset(xn_lo[:, :, D - 1:D], 0.0).then_inc(prep_p, 1)
            pool.memset(mcol[:, :, :, :], 0.0).then_inc(prep_p, 1)
            pool.wait_ge(prep_p, 5)
            pool.memset(head_ops[64:128, :, 1, :], 0.0).then_inc(prep_p, 1)
            pool.wait_ge(prep_p, 6)
            pool.memset(head_ops[64:128, :, 3, :], 0.0).then_inc(prep_p, 1)
            pool.wait_ge(prep_p, 7)
            pool.memset(head_ops[64:65, :, 3, :], 1.0).then_inc(prep_p, 1)
            pool.wait_ge(prep_v, 2)
            pool.wait_ge(prep_p, 8)
            pool.partition_all_reduce(pow2[:, 0:3], amax[:, 0:3], 128, RMAX).then_inc(prep_p, 1)
            pool.wait_ge(prep_a, 3)
            pool.wait_ge(prep_p, 9)
            pool.tensor_tensor(w_lo[:, :, :], qk32[:, :, :], w_hi[:, :, :], ALU.subtract).then_inc(prep_p, 1)
            pool.wait_ge(prep_a, 5)
            pool.tensor_tensor(vo_lo[:, :, :], vo32[:, :, :], vo_hi[:, :, 0:D], ALU.subtract).then_inc(prep_p, 1)
            for b in range(B):
                tiles = slice(b * TT, (b + 1) * TT)
                pool.wait_ge(xnh_ready, b + 1)
                pool.tensor_tensor(xn_lo[:, tiles, 0:D - 1], xhat[:, tiles, 0:D - 1], xn_hi[:, tiles, 0:D - 1],
                                   ALU.subtract).then_inc(xnl_ready, 1)

            def p_low(k, par, a):
                pool.wait_ge(phi_done, 2 * k + (a + 1))
                rows = slice(2 * a, 2 * a + 2)
                pool.tensor_tensor(p_lo[:, par, rows, :], p32[:, par, rows, :], p_hi[:, par, rows, :],
                                   ALU.subtract).then_inc(plo_done, 1)

            for a in range(2):
                p_low(0, 0, a)
            for a in range(2):
                p_low(1, 1, a)
            with pool.Fori(0, NH // 2 - 1) as i:
                for j in range(2):
                    k = 2 * i + (j + 2)
                    for a in range(2):
                        pool.wait_ge(av_half, 2 * (k - 2) + (a + 1))
                        p_low(k, j, a)

        @block.scalar
        def _(act):
            act.dma_start(scl[0:16, :, :], sc_d[0].partition_broadcast(16)).then_inc(sc_in, 16)
            for s in range(1, G):
                act.dma_start(scl[16 * s:16 * s + 16, :, :], sc_d[s].partition_broadcast(16)).then_inc(sc_in, 16)

            act.wait_ge(consts, 3)
            nc.scalar.activation(ident16[:, :], ident[:, :], ACT.Copy).then_inc(prep_a, 1)

            def pre(f, s):
                for c in range(SG):
                    b = s * SG + c
                    act.wait_ge(pre_t, f * B + b + 1)
                    nc.scalar.activation(hT[:, b, :], bank[b], ACT.Copy).then_inc(h_ready, 1)

            def norm_apply(u, s):
                act.wait_ge(moments_ready, u + 1)
                for c in range(SG // 2, SG):
                    for t in range(c * TT, (c + 1) * TT):
                        ins = nc.scalar.activation(xhat[:, s * GT + t, :], x[:, s * GT + t, :], ACT.Identity,
                                                   scale=rstd[:, s, t:t + 1], bias=shift[:, s, t:t + 1])
                    ins.then_inc(xhat_a, 1)

            def at(f, n, s, c):
                return ((f * NB + n) * 2 + s) * SG + c + 1

            def centre(f, n, s):
                for c in range(SG):
                    b = s * SG + c
                    act.wait_ge(lin1_done, at(f, n, s, c))
                    nc.scalar.activation(work_a[:, b, :], bank[b], ACT.Identity,
                                         bias=bias_c[:, 2 * n:2 * n + 1]).then_inc(yc_ready, 1)
                    nc.scalar.activation(work_b[:, b, :], bank[b], ACT.Square,
                                         bias=bias_c[:, 2 * n:2 * n + 1]).then_inc(sq_ready, 1)

            def gelu(f, n, s):
                for c in range(SG):
                    b = s * SG + c
                    act.wait_ge(z_ready, at(f, n, s, c))
                    nc.scalar.activation(work_a[:, b, :], work_b[:, b, :], ACT.Gelu, scale=gam[:, n:n + 1],
                                         bias=bet[:, n:n + 1]).then_inc(gl_ready, 1)

            def weight_halves():
                act.wait_ge(prep_v, 3)
                for n in range(2):
                    nc.scalar.activation(w_hi[:, n, :], qk32[:, n, :], ACT.Identity, scale=inv2[:, n:n + 1])
                ins = nc.scalar.activation(vo_hi[:, :, 0:D], vo32[:, :, :], ACT.Identity, scale=inv2[:, 2:3])
                ins.then_inc(prep_a, 1)
                act.wait_ge(prep_a, 2)
                for n in range(2):
                    ins = nc.scalar.activation(qk32[:, n, :], qk32[:, n, :], ACT.Identity, scale=inv2[:, n:n + 1])
                ins.then_inc(prep_a, 1)
                nc.scalar.activation(vo_hi[:, :, D:D + 1].rearrange("p h a -> p (h a)"),
                                     ident[:, D - 1:D].to_broadcast([128, H]), ACT.Identity,
                                     scale=inv2[:, 2:3]).then_inc(prep_a, 1)
                nc.scalar.activation(vo32[:, :, :], vo32[:, :, :], ACT.Identity, scale=inv2[:, 2:3]).then_inc(prep_a, 1)

            def halves_tokens(u, b):
                wait_xhat(act, u, b % SG)
                tiles = slice(b * TT, (b + 1) * TT)
                nc.scalar.activation(xn_hi[:, tiles, 0:D - 1], xhat[:, tiles, 0:D - 1], ACT.Copy).then_inc(xnh_ready, 1)

            def halves_turned(b, src):
                act.wait_ge(xn_t, b + 1)
                nc.scalar.activation(xt_hi[:, b, :], src, ACT.Copy).then_inc(xth_ready, 1)

            def ffn(f):
                if f == 0:
                    norm_apply(0, 0)
                pre(f, 0)
                if f == 0:
                    act.wait_ge(prep_v, 1)
                for n in range(NB):
                    centre(f, n, 0)
                    if n:
                        gelu(f, n - 1, 1)
                    else:
                        norm_apply(4 * f + 1, 1)
                        pre(f, 1)
                    gelu(f, n, 0)
                    centre(f, n, 1)
                    if f == 0 and n == 1:
                        weight_halves()
                gelu(f, NB - 1, 1)
                if f == 0:
                    norm_apply(2, 0)
                    for b in range(SG):
                        halves_turned(b, bank[b])
                    for b in range(SG):
                        halves_tokens(2, b)

            ffn(0)

            def q_high(pair):
                act.wait_ge(q_proj, pair + 1)
                nc.scalar.activation(pair_ops[:, 0, :], qj_ps, ACT.Copy).then_inc(qh_ready, 1)

            def k_high(pair):
                act.wait_ge(k_proj, pair + 1)
                nc.scalar.activation(pair_ops[:, 2, :], kj_ps, ACT.Copy).then_inc(kh_ready, 1)

            def row_max(k, ring):
                act.wait_ge(m_turned, k + 1)
                nc.scalar.activation(q2[64:128, ring, :], qj_ps[64:128, :], ACT.Copy).then_inc(m_ready, 1)

            def exps(k, par, a):
                act.wait_ge(s_done, 2 * k + (a + 1))
                nc.scalar.activation(p32[:, par, 2 * a:2 * a + 2, :], s_ps[a], ACT.Exp,
                                     scale=exp_scale[:, 0:1]).then_inc(exp_done, 1)

            def p_high(k, par, a):
                act.wait_ge(exp_done, 2 * k + (a + 1))
                nc.scalar.activation(p_hi[:, par, 2 * a:2 * a + 2, :], p32[:, par, 2 * a:2 * a + 2, :],
                                     ACT.Copy).then_inc(phi_done, 1)

            def y_high(k):
                act.wait_ge(av_half, 2 * k + 2)
                nc.scalar.activation(y_hi[:, :], y_ps, ACT.Copy).then_inc(yh_ready, 1)

            def spread_over(pair):
                act.wait_ge(spread_done[0], 64 * pair)
                act.wait_ge(spread_done[1], 64 * pair)
                act.wait_ge(q2_spread, 32 * pair)

            def slot(k, j, lo, hi):
                if lo >= -1 and hi + 1 < NH:
                    for a in range(2):
                        if lo + 1 >= 2:
                            act.wait_ge(plo_done, 2 * (k - 1) + (a + 1))
                        exps(k + 1, (j + 1) % 2, a)
                    if lo + 1 >= 2:
                        act.wait_ge(av_half, 2 * (k - 1) + 1)
                    p_high(k + 1, (j + 1) % 2, 0)
                if lo >= -2 and hi + 2 < NH:
                    row_max(k + 2, (j + 2) % 4)
                if lo >= -1 and hi + 1 < NH:
                    if lo + 1 >= 2:
                        act.wait_ge(av_half, 2 * (k - 1) + 2)
                    p_high(k + 1, (j + 1) % 2, 1)
                if j % 2 == 0 and hi + 4 < NH:
                    pair = (k + 4) // 2 if isinstance(k, int) else pair_of(k, j)
                    if lo > -4:
                        spread_over(pair)
                    q_high(pair)
                    k_high(pair)
                if lo >= 0:
                    if lo >= 1:
                        act.wait_ge(o_done, k)
                    y_high(k)

            quad = [None]

            def pair_of(k, j):
                return 2 * quad[0] + (j // 2 + 2)

            for k in range(-4, 4):
                slot(k, k % 4, k, k)
                if k == -3:
                    norm_apply(3, 1)
                    for b in range(SG, B):
                        halves_tokens(3, b)
                if k in (-2, -1):
                    for b in late_turns(k):
                        halves_turned(b, late_bank(b))
            with act.Fori(1, NH // 4 - 1) as i:
                quad[0] = i
                for j in range(4):
                    slot(4 * i + j, j, 4 + j, NH - 8 + j)
            for k in range(NH - 4, NH):
                slot(k, k % 4, k, k)
                if k == NH - 2:
                    norm_apply(4, 0)

            ffn(1)

        @block.vector
        def _(dve):
            link = Link()

            def rsqrt(src, y):
                link(dve, nc.vector.tensor_scalar(var[:, :], src, LN_EPS, None, ALU.add))
                link(dve, nc.vector.tensor_scalar(y.bitcast(I32), var[:, :].bitcast(I32), -0.5, MAGIC,
                                                  ALU.mult, ALU.add))
                for step in range(3):
                    link(dve, nc.vector.scalar_tensor_tensor(rs_t[:, :], y, -0.5, y, ALU.mult, ALU.mult))
                    link(dve, nc.vector.tensor_tensor(rs_u[:, :], rs_t[:, :], var[:, :], ALU.mult))
                    last = nc.vector.scalar_tensor_tensor(y, rs_u[:, :], 1.5, y, ALU.add, ALU.mult)
                    if step < 2:
                        link(dve, last)
                return last

            def weight_maxima():
                dve.wait_ge(a_in, 16 * 4)
                nc.vector.tensor_reduce(amax[:, 0:1], qk32[:, 0, :], AX.X, ALU.max, apply_absolute_value=True)
                nc.vector.tensor_reduce(amax[:, 1:2], qk32[:, 1, :], AX.X, ALU.max, apply_absolute_value=True)
                dve.wait_ge(prep_p, 2)
                link(dve, nc.vector.tensor_reduce(amax[:, 2:3], vo32[:, :, :].rearrange("p h d -> p (h d)"), AX.X,
                                                  ALU.max, apply_absolute_value=True))
                nc.vector.tensor_scalar(amax[:, 0:3], amax[:, 0:3], 1e-30, None, ALU.max).then_inc(prep_v, 1)

            def weight_scales():
                dve.wait_ge(prep_p, 9)
                link(dve, nc.vector.tensor_scalar(pow2[:, 0:3].bitcast(I32), pow2[:, 0:3].bitcast(I32), EXPONENT,
                                                  None, ALU.bitwise_and))
                link(dve, nc.vector.tensor_scalar(inv2[:, 0:3].bitcast(I32), pow2[:, 0:3].bitcast(I32), -1.0,
                                                  ONE_BITS2, ALU.mult, ALU.add))
                link(dve, nc.vector.tensor_scalar(inv2[:, 0:2], inv2[:, 0:2], QK_TOP, None, ALU.mult))
                link(dve, nc.vector.tensor_scalar(inv2[:, 2:3], inv2[:, 2:3], VO_CLAMP, 1.0 / VO_CLAMP,
                                                  ALU.min, ALU.max))
                nc.vector.tensor_scalar(exp_scale[:, :], pow2[:, 0:1], pow2[:, 1:2],
                                        1.0 / (QK_TOP * QK_TOP * float(D) ** 0.5), ALU.mult,
                                        ALU.mult).then_inc(prep_v, 1)

            def norm_stats(batches, loaded=False):
                for b in batches:
                    if loaded:
                        dve.wait_ge(x_in[b], 16)
                    for t in range(b * TT, (b + 1) * TT):
                        ins = nc.vector.bn_stats(stats[:, t % GT, :], x[:, t, :])
                link(dve, ins)

            def norm_moments(s):
                for t in range(GT):
                    ins = nc.vector.bn_aggr(mv[:, s, t, :], stats[:, t, :])
                link(dve, ins)
                link(dve, rsqrt(mv[:, s, :, 1], rstd[:, s, :]))
                nc.vector.scalar_tensor_tensor(shift[:, s, :], mv[:, s, :, 0], -1.0, rstd[:, s, :], ALU.mult,
                                               ALU.mult).then_inc(moments_ready, 1)

            def norm_apply(s):
                for c in range(SG // 2):
                    for t in range(c * TT, (c + 1) * TT):
                        ins = nc.vector.tensor_scalar(xhat[:, s * GT + t, :], x[:, s * GT + t, :], mv[:, s, t, 0:1],
                                                      rstd[:, s, t:t + 1], ALU.subtract, ALU.mult)
                    ins.then_inc(xhat_v, 1)

            norm_stats(range(SG), loaded=True)
            norm_moments(0)
            norm_apply(0)

            dve.wait_ge(w_in, 16 * 6)
            link(dve, nc.vector.tensor_scalar(wt[:, :, :], qw[:, :, :], 1.0 / 7.5, -1.0, ALU.mult, ALU.add))
            dve.wait_ge(sc_in, 16 * G)
            link(dve, nc.vector.tensor_tensor(wt[:, :, :], wt[:, :, :], scl[:, :, :], ALU.mult))
            dve.wait_ge(prep_pe, 1)
            for b in range(2):
                half = slice(3 * b, 3 * b + 3)
                ins = nc.vector.tensor_tensor(
                    wt[:, half, :], ps[:, SG + b, 0:3 * D].rearrange("p (n d) -> p n d", n=3), wt[:, half, :], ALU.add)
                link(dve, ins)
            link(dve, nc.vector.tensor_reduce(wmean[:, :], wt[:, :, :], AX.X, ALU.add))
            link(dve, nc.vector.tensor_scalar(wmean[:, :], wmean[:, :], -1.0 / D, None, ALU.mult))
            for n in range(0, NL, 2):
                link(dve, nc.vector.tensor_scalar(wt[:, n, :], wt[:, n, :], wmean[:, n:n + 1], None, ALU.add))
            link(dve, nc.vector.tensor_copy(bias_c[:, :], bias[:, :]))
            nc.vector.tensor_tensor(bias_c[:, 0:NL:2], bias[:, 0:NL:2], ps[:, SG + 2, 0:NL:2],
                                    ALU.subtract).then_inc(prep_v, 1)

            def at(f, n, s, c):
                return ((f * NB + n) * 2 + s) * SG + c + 1

            def step_rsqrt(f, n, s):
                dve.wait_ge(var_done, at(f, n, s, SG - 1))
                rsqrt(bank[s * SG][:, 0:GT], rstd[:, s, :]).then_inc(rstd_ready, 1)

            def step_z(f, n, s):
                for c in range(SG):
                    b = s * SG + c
                    dve.wait_ge(yc_ready, at(f, n, s, c))
                    dve.wait_ge(rb_done, at(f, n, s, c))
                    nc.vector.tensor_tensor(work_b[:, b, :], bank[b], work_a[:, b, :],
                                            ALU.mult).then_inc(z_ready, 1)

            def step_h(f, n, s):
                for c in range(SG):
                    b = s * SG + c
                    dve.wait_ge(lin2_done, at(f, n, s, c))
                    nc.vector.scalar_tensor_tensor(hT[:, b, :], bank[b], bias[:, 2 * n + 1:2 * n + 2], hT[:, b, :],
                                                   ALU.add, ALU.add).then_inc(h_ready, 1)

            def step_x(f, s):
                for c in range(SG):
                    b = s * SG + c
                    dve.wait_ge(post_t, f * B + b + 1)
                    rows = x[:, b * TT:(b + 1) * TT, :].rearrange("p a d -> p (a d)")
                    ins = nc.vector.scalar_tensor_tensor(rows, bank[b], 0.5, rows, ALU.mult, ALU.add)
                    ins.then_inc(x1_ready, 1)

            def split(b, src):
                dve.wait_ge(xth_ready, b + 1)
                nc.vector.tensor_tensor(xt_lo[:, b, :], src, xt_hi[:, b, :], ALU.subtract).then_inc(xsplit_done, 1)

            def ffn(f):
                if f:
                    norm_stats([B - 1])
                else:
                    norm_stats(range(SG, B), loaded=True)
                norm_moments(1)
                norm_apply(1)
                for n in range(NB):
                    if n:
                        step_z(f, n - 1, 1)
                    step_rsqrt(f, n, 0)
                    if n:
                        step_h(f, n - 1, 1)
                    step_z(f, n, 0)
                    if f == 0 and n == 0:
                        weight_maxima()
                    step_h(f, n, 0)
                    if f == 0 and n == 0:
                        weight_scales()
                    step_rsqrt(f, n, 1)
                step_x(f, 0)
                step_z(f, NB - 1, 1)
                if f == 0:
                    dve.wait_ge(x1_ready, SG)
                    norm_stats(range(SG))
                    norm_moments(0)
                    norm_apply(0)
                step_h(f, NB - 1, 1)
                step_x(f, 1)
                if f == 0:
                    for b in range(SG):
                        split(b, bank[b])

            ffn(0)

            ADD_LINKS = 1

            def q_low(pair):
                dve.wait_ge(qh_ready, pair + 1)
                nc.vector.tensor_tensor(pair_ops[:, 1, :], qj_ps, pair_ops[:, 0, :], ALU.subtract).then_inc(ql_ready, 1)

            def k_low(pair):
                dve.wait_ge(kh_ready, pair + 1)
                nc.vector.tensor_tensor(pair_ops[:, 3, :], kj_ps, pair_ops[:, 2, :], ALU.subtract).then_inc(kl_ready, 1)

            def reduce_max(k, par, a):
                dve.wait_ge(max_mm, 2 * k + (a + 1))
                nc.vector.tensor_reduce(mcol[:, par, 2 * a:2 * a + 2, R], s_ps[a], AX.X, ALU.max,
                                        negate=True).then_inc(max_red, 1)

            def y_low(k):
                dve.wait_ge(yh_ready, k + 1)
                nc.vector.tensor_tensor(y_lo[:, :], y_ps, y_hi[:, :], ALU.subtract).then_inc(yl_ready, 1)

            def add_out(mine, k, batch):
                dve.wait_ge(o_done, k + 1)
                mine(dve, nc.vector.reciprocal(rinv[:, :].rearrange("p (a b) -> p a b", a=2), o_ps[:, :, :, D]))
                for t in range(TT):
                    row = x[:, bass.ds(batch * TT + t, 1), :].rearrange("p a d -> p (a d)")
                    ins = nc.vector.scalar_tensor_tensor(row, o_ps[:, t // 2, t % 2, 0:D], rinv[:, t:t + 1], row,
                                                         ALU.mult, ALU.add)
                ins.then_inc(o_added, 1)

            def slot(mine, i, k, j, lo, hi):
                if lo >= 1 and lo - 1 < NH:
                    if lo >= 2:
                        dve.wait_ge(o_added, k - 1)
                    add_out(mine, k - 1, (i * 4 + (j - 1)) // H)
                if lo >= -3 and hi + 3 < NH:
                    maxima(k, j, lo, 0)
                    maxima(k, j, lo, 1)
                pair = 2 * i + (j // 2 + 2)
                if j % 2 == 0 and hi + 4 < NH:
                    if lo > -4:
                        dve.wait_ge(spread_done[0], 64 * pair)
                        dve.wait_ge(spread_done[1], 64 * pair)
                        dve.wait_ge(q2_spread, 32 * pair)
                    q_low(pair)
                    k_low(pair)
                if 0 <= lo and hi < NH:
                    y_low(k)

            def maxima(k, j, lo, a):
                if lo + 3 >= 2 and a == 0:
                    dve.wait_ge(m_turned, k + 2)
                reduce_max(k + 3, (j + 3) % 2, a)

            for k in range(-4, 4):
                slot(link, k // 4, k, k % 4, k, k)
                if k == -4:
                    dve.wait_ge(x1_ready, B)
                    norm_stats(range(SG, B))
                if k == -3:
                    norm_moments(1)
                    norm_apply(1)
                if k in (-2, -1):
                    for b in late_turns(k):
                        split(b, late_bank(b))
            start = link.base + link.n
            with dve.Fori(1, NH // 4 - 1) as i:
                mine = Link()
                mine.base = i * (4 * ADD_LINKS) + (start - 4 * ADD_LINKS)
                for j in range(4):
                    slot(mine, i, 4 * i + j, j, 4 + j, NH - 8 + j)
            link.base, link.n = start + (NH // 4 - 2) * 4 * ADD_LINKS, 0
            for k in range(NH - 4, NH + 1):
                slot(link, k // 4, k, k % 4, k, k)
                if k == NH - 4:
                    norm_stats(range(SG))
                if k == NH - 3:
                    norm_moments(0)
                if k == NH - 2:
                    norm_apply(0)
                if k == NH - 1:
                    norm_stats(range(SG, B - 1))
            dve.wait_ge(o_added, NH)

            ffn(1)

        @block.tensor
        def _(pe):
            pe.wait_ge(w_in, 16 * 6)
            pe.wait_ge(consts, 3)
            nc.tensor.matmul(ps[:, SG + 2, 0:NL], mean_mat[:, :], bias[:, :], start=True, stop=True)
            for n in range(NL):
                ins = nc.tensor.matmul(ps[:, SG + n // 3, (n % 3) * D:(n % 3 + 1) * D], la[:, n, :], lb[:, n, :],
                                       start=True, stop=True)
            ins.then_inc(prep_pe, 1)

            def turn(dst, src, done):
                for t in range(TT):
                    ins = nc.tensor.transpose(dst[:, t * 128:(t + 1) * 128], src(t), ident[:, :])
                ins.then_inc(done, 1)

            def at(f, n, s, c):
                return ((f * NB + n) * 2 + s) * SG + c + 1

            def batches(s):
                return [(c, s * SG + c) for c in range(SG)]

            def pre(f, s):
                for c, b in batches(s):
                    wait_xhat(pe, 4 * f + s, c)
                    turn(bank[b], lambda t: xhat[:, b * TT + t, :], pre_t)

            def lin1(f, n, s):
                for c, b in batches(s):
                    pe.wait_ge(h_ready, f * (NB + 1) * B + (b + 1 if n == 0 else B + ((n - 1) * 2 + s) * SG + c + 1))
                    nc.tensor.matmul(bank[b], wt[:, 2 * n, :], hT[:, b, :], start=True, stop=True).then_inc(lin1_done, 1)

            def variance(f, n, s):
                for c, b in batches(s):
                    pe.wait_ge(sq_ready, at(f, n, s, c))
                    for t in range(TT):
                        col = c * TT + t
                        ins = nc.tensor.matmul(bank[s * SG][:, col:col + 1], work_b[:, b, t * 128:(t + 1) * 128],
                                               ones_col[:, :], start=True, stop=True)
                    ins.then_inc(var_done, 1)

            def spread_rstd(f, n, s):
                pe.wait_ge(rstd_ready, (f * NB + n) * 2 + s + 1)
                for c, b in batches(s):
                    for t in range(TT):
                        col = c * TT + t
                        ins = nc.tensor.matmul(bank[b][:, t * 128:(t + 1) * 128],
                                               rstd[:, s, col:col + 1].to_broadcast([128, 128]), ident[:, :],
                                               start=True, stop=True)
                    ins.then_inc(rb_done, 1)

            def lin2(f, n, s):
                for c, b in batches(s):
                    pe.wait_ge(gl_ready, at(f, n, s, c))
                    nc.tensor.matmul(bank[b], wt[:, 2 * n + 1, :], work_a[:, b, :], start=True,
                                     stop=True).then_inc(lin2_done, 1)

            def post(f, s):
                for c, b in batches(s):
                    pe.wait_ge(h_ready, f * (NB + 1) * B + B + ((NB - 1) * 2 + s) * SG + c + 1)
                    turn(bank[b], lambda t: hT[:, b, t * 128:(t + 1) * 128], post_t)

            def turn_xn(u, b, dst):
                wait_xhat(pe, u, b % SG)
                turn(dst, lambda t: xhat[:, b * TT + t, :], xn_t)

            def ffn(f):
                if f == 0:
                    pre(0, 0)
                    pe.wait_ge(prep_v, 1)
                for n in range(NB):
                    lin1(f, n, 0)
                    if n:
                        spread_rstd(f, n - 1, 1)
                    variance(f, n, 0)
                    if n:
                        lin2(f, n - 1, 1)
                    else:
                        pre(f, 1)
                    spread_rstd(f, n, 0)
                    lin1(f, n, 1)
                    lin2(f, n, 0)
                    variance(f, n, 1)
                post(f, 0)
                spread_rstd(f, NB - 1, 1)
                lin2(f, NB - 1, 1)
                if f == 0:
                    for b in range(SG):
                        turn_xn(2, b, bank[b])
                post(f, 1)

            ffn(0)

            pe.wait_ge(prep_a, 5)
            pe.wait_ge(prep_p, 11)
            pe.wait_ge(xsplit_done, 1)

            def project(dst, which, pair, col, batch, done):
                hi = w_hi[:, which, bass.ds(col, 128)]
                lo = w_lo[:, which, bass.ds(col, 128)]
                xh = xt_hi[:, bass.ds(batch, 1), :].rearrange("p a t -> p (a t)")
                xl = xt_lo[:, bass.ds(batch, 1), :].rearrange("p a t -> p (a t)")
                nc.tensor.matmul(dst, hi, xh, start=True, stop=False)
                nc.tensor.matmul(dst, hi, xl, start=False, stop=False)
                nc.tensor.matmul(dst, lo, xh, start=False, stop=True).then_inc(done, 1)

            def maxima(k, ring, a):
                for t in (2 * a, 2 * a + 1):
                    ins = nc.tensor.matmul(s_ps[a][:, t % 2, :], q1[:, ring, t * 128:(t + 1) * 128], k1[:, ring, :],
                                           start=True, stop=True)
                ins.then_inc(max_mm, 1)

            def turn_max(k, par):
                for t in range(TT):
                    ins = nc.tensor.matmul(qj_ps[:, t * 128:(t + 1) * 128], mcol[:, par, t, :], ident16[:, :],
                                           start=True, stop=True)
                ins.then_inc(m_turned, 1)

            def scores(k, ring, a):
                for u in (2 * a, 2 * a + 1):
                    keys = slice(u * 128, (u + 1) * 128)
                    nc.tensor.matmul(s_ps[a][:, u % 2, :], k1[:, ring, keys], q1[:, ring, :], start=True, stop=False)
                    ins = nc.tensor.matmul(s_ps[a][:, u % 2, :], k2[:, ring, keys], q2[:, ring, :],
                                           start=False, stop=True)
                ins.then_inc(s_done, 1)

            def weigh(par, a, batch):
                for u in (2 * a, 2 * a + 1):
                    row = bass.ds(batch * TT + u, 1)
                    xh = xn_hi[:, row, :].rearrange("p a d -> p (a d)")
                    xl = xn_lo[:, row, :].rearrange("p a d -> p (a d)")
                    nc.tensor.matmul(y_ps, xh, p_hi[:, par, u, :], start=(u == 0), stop=False)
                    nc.tensor.matmul(y_ps, xl, p_hi[:, par, u, :], start=False, stop=False)
                    ins = nc.tensor.matmul(y_ps, xh, p_lo[:, par, u, :], start=False, stop=(u == TT - 1))
                ins.then_inc(av_half, 1)

            def outputs(head):
                vh = vo_hi[:, bass.ds(head, 1), 0:RW].rearrange("p a d -> p (a d)")
                vl = vo_lo[:, bass.ds(head, 1), :].rearrange("p a d -> p (a d)")
                for t in range(TT):
                    cols = slice(t * 128, (t + 1) * 128)
                    o = o_ps[:, t // 2, t % 2, :]
                    nc.tensor.matmul(o, y_hi[:, cols], vh, start=True, stop=False)
                    nc.tensor.matmul(o[:, 0:D], y_hi[:, cols], vl, start=False, stop=False)
                    ins = nc.tensor.matmul(o, y_lo[:, cols], vh, start=False, stop=True)
                ins.then_inc(o_done, 1)

            QPB = H // 4

            def slot(i, k, j, lo, hi):
                pair = 2 * i + (j // 2 + 2)
                pj_head = ((i + 1) % QPB) * 4 + j
                if lo >= -1 and hi + 1 < NH:
                    pe.wait_ge(m_ready, k + 2)
                    pe.wait_ge(q2_spread, 32 * (2 * i + ((j + 1) // 2 + 1)))
                    if hi + 2 < NH:
                        pe.wait_ge(max_red, 2 * k + 5)
                    else:
                        pe.wait_ge(exp_done, 2 * k + 1)
                    scores(k + 1, (j + 1) % 4, 0)
                    if hi + 2 < NH:
                        pe.wait_ge(max_red, 2 * k + 6)
                    else:
                        pe.wait_ge(exp_done, 2 * k + 2)
                    scores(k + 1, (j + 1) % 4, 1)
                if lo >= -2 and hi + 2 < NH:
                    pe.wait_ge(max_red, 2 * k + 6)
                    pe.wait_ge(ql_ready, pairs_so_far(i, j, k))
                    turn_max(k + 2, j % 2)
                if lo >= 1:
                    pe.wait_ge(yl_ready, k)
                    if lo >= 2:
                        pe.wait_ge(o_added, k - 1)
                    pe.wait_ge(kl_ready, pairs_so_far(i, j, k))
                    outputs((4 * i + (j - 1)) % H)
                if 0 <= lo < NH:
                    pe.wait_ge(plo_done, 2 * k + 1)
                    weigh(j % 2, 0, i // QPB)
                all_maxima(i, k, j, lo, hi)
                if j % 2 == 0 and hi + 4 < NH:
                    if lo >= -2:
                        pe.wait_ge(m_ready, k + 3)
                    project(qj_ps, 0, pair, pj_head * R, (i + 1) // QPB, q_proj)
                    if lo >= 1:
                        pe.wait_ge(o_added, k)
                    project(kj_ps, 1, pair, pj_head * R, (i + 1) // QPB, k_proj)
                if 0 <= lo < NH:
                    pe.wait_ge(plo_done, 2 * k + 2)
                    weigh(j % 2, 1, i // QPB)

            def all_maxima(i, k, j, lo, hi):
                if lo >= -3 and hi + 3 < NH:
                    pe.wait_ge(spread_done[(j + 3) % 2], 64 * spread_pairs(i, j))
                    if lo >= -1:
                        pe.wait_ge(exp_done, 2 * k + 3)
                    if lo + 2 >= 0:
                        pe.wait_ge(max_red, 2 * k + 5)
                    maxima(k + 3, (j + 3) % 4, 0)
                    if lo >= -1:
                        pe.wait_ge(exp_done, 2 * k + 4)
                    if lo + 2 >= 0:
                        pe.wait_ge(max_red, 2 * k + 6)
                    maxima(k + 3, (j + 3) % 4, 1)

            def pairs_so_far(i, j, k):
                n = 2 * i + ((j + 3) // 2 + 1)
                return n if not isinstance(n, int) else min(n, NH // 2)

            def spread_pairs(i, j):
                return 2 * i + ((j + 3) // 2 + 1)

            for k in range(-4, 4):
                slot(k // 4, k, k % 4, k, k)
                if k == -4:
                    pe.wait_ge(xsplit_done, SG)
                if k in (-2, -1):
                    for b in late_turns(k):
                        if k == -1:
                            pe.wait_ge(xsplit_done, b - 1)
                        turn_xn(3, b, late_bank(b))
                if k == -1:
                    pe.wait_ge(xnl_ready, SG)
                    pe.wait_ge(xsplit_done, B)
            pe.wait_ge(xnl_ready, B)
            with pe.Fori(1, NH // 4 - 1) as i:
                for j in range(4):
                    slot(i, 4 * i + j, j, 4 + j, NH - 8 + j)
            for k in range(NH - 4, NH + 1):
                slot(k // 4, k, k % 4, k, k)
                if k == NH - 1:
                    pre(1, 0)
            pe.wait_ge(o_added, NH)

            ffn(1)


def kernel(**inputs):
    import numpy as np
    import concourse.bacc as bacc
    from concourse.bass_utils import run_bass_kernel_spmd

    a = {n: np.asarray(v) for n, v in inputs.items()}
    D = a["L0_attn_x"].shape[2]
    arrays = {
        "x": a["L0_attn_x"],
        "wq": a["L0_attn_Q"].transpose(2, 0, 1).reshape(D, -1),
        "wk": a["L0_attn_K"].transpose(2, 0, 1).reshape(D, -1),
        "wvo": a["L0_attn_VO"],
        "qweights": a["L0_ffn_qweights"].transpose(2, 0, 1),
        "scales": a["L0_ffn_scales"].transpose(2, 0, 1),
        "biases": a["L0_ffn_biases"].T,
        "lora_a": a["L0_ffn_lora_a"].transpose(1, 0, 2),
        "lora_b": a["L0_ffn_lora_b"].transpose(2, 0, 1),
        "ln_gamma": a["L0_ffn_ln_gamma"].T,
        "ln_beta": a["L0_ffn_ln_beta"].T,
    }
    arrays = {n: np.ascontiguousarray(v) for n, v in arrays.items()}
    nc = bacc.Bacc("TRN2", target_bir_lowering=False, num_devices=1)
    args = [nc.dram_tensor(n + "_dram", v.shape, mybir.dt.from_np(v.dtype), kind="ExternalInput").ap()
            for n, v in arrays.items()]
    out = nc.dram_tensor("out", a["L0_attn_x"].shape, F32, kind="ExternalOutput").ap()
    macaron(nc, *args, out)
    r = run_bass_kernel_spmd(nc, [{n + "_dram": v for n, v in arrays.items()}], core_ids=[0])
    return r.results[0]["out"]
```
